# Optimizing a Trainium2 kernel written in Bass

```python
import numpy as np
import jax
import jax.numpy as jnp

def _softmax(x, axis=-1):
    return jax.nn.softmax(x, axis=axis)

def _gelu(x):
    return jax.nn.gelu(x, approximate=True)

def _silu(x):
    return jax.nn.silu(x)

def _sigmoid(x):
    return jax.nn.sigmoid(x)

def _layernorm(x, axis=-1, eps=1e-05):
    m = jnp.mean(x, axis=axis, keepdims=True)
    v = jnp.var(x, axis=axis, keepdims=True)
    return (x - m) / jnp.sqrt(v + eps)

def _scatter_add(tgt, idx, src, axis=0):
    return tgt.at[idx].add(src)

def _segment_sum(src, seg, n):
    return jax.ops.segment_sum(src, seg, n)
kernel_name = 'mk_adaln_d1_jaxref_r4_0bc225'

def setup_inputs(seed: int=0):
    np.random.seed(seed)
    _w = jnp.asarray

    def _L0_attn_setup():
        import jax, jax.numpy as jnp
        import numpy as np
        D_MODEL = 256
        N_HEAD = 8
        D_X = 64
        EPS = 1e-06
        key = jax.random.key(seed)
        ks = jax.random.split(key, 7)
        B, L = (4, 2048)
        x = jax.random.normal(ks[0], (B, L, D_MODEL), dtype=jnp.float32)
        s_qkv = 1.0 / np.sqrt(D_MODEL)
        w_qkv = jax.random.uniform(ks[1], (D_MODEL, 3 * N_HEAD * D_X), dtype=jnp.float32, minval=-s_qkv, maxval=s_qkv)
        b_qkv = jax.random.uniform(ks[2], (3 * N_HEAD * D_X,), dtype=jnp.float32, minval=-s_qkv, maxval=s_qkv)
        s_fc = 1.0 / np.sqrt(N_HEAD * D_X)
        w_fc = jax.random.uniform(ks[3], (N_HEAD * D_X, D_MODEL), dtype=jnp.float32, minval=-s_fc, maxval=s_fc)
        b_fc = jax.random.uniform(ks[4], (D_MODEL,), dtype=jnp.float32, minval=-s_fc, maxval=s_fc)
        gamma = jnp.ones((D_MODEL,), dtype=jnp.float32)
        beta = jnp.zeros((D_MODEL,), dtype=jnp.float32)
        return {'x': x, 'w_qkv': w_qkv, 'b_qkv': b_qkv, 'w_fc': w_fc, 'b_fc': b_fc, 'gamma': gamma, 'beta': beta}
    _L0_attn_in = _L0_attn_setup()

    def _L0_ffn_setup():
        import jax, jax.numpy as jnp
        import numpy as np
        DIM = 256

        def _reference_tuple_inner(x, W_r, W_k, W_v, mu_r, mu_k):
            B, T, C = x.shape
            x_prev = jnp.concatenate([jnp.zeros((B, 1, C), x.dtype), x[:, :-1, :]], axis=1)
            xr = mu_r * x + (1.0 - mu_r) * x_prev
            xk = mu_k * x + (1.0 - mu_k) * x_prev
            r = jax.nn.sigmoid(jnp.einsum('btc,dc->btd', xr, W_r))
            k = jnp.einsum('btc,dc->btd', xk, W_k)
            k_act = jnp.square(jax.nn.relu(k))
            out = r * jnp.einsum('btc,dc->btd', k_act, W_v)
            new_state = x[:, -1, :]
            return (out, new_state)
        key = jax.random.key(seed)
        ks = jax.random.split(key, 6)
        B, T, C = (8, 512, DIM)
        x = jax.random.normal(ks[0], (B, T, C), dtype=jnp.float32)
        s = 1.0 / np.sqrt(C)
        W_r = jax.random.uniform(ks[1], (C, C), jnp.float32, -s, s)
        W_k = jax.random.uniform(ks[2], (C, C), jnp.float32, -s, s)
        W_v = jax.random.uniform(ks[3], (C, C), jnp.float32, -s, s)
        mu_r = jax.random.uniform(ks[4], (C,), jnp.float32)
        mu_k = jax.random.uniform(ks[5], (C,), jnp.float32)
        return {'x': x, 'W_r': W_r, 'W_k': W_k, 'W_v': W_v, 'mu_r': mu_r, 'mu_k': mu_k}
    _L0_ffn_in = _L0_ffn_setup()
    _L0_c = _w((lambda *s: np.random.randn(*s).astype(np.float32) * 0.05)(8, 256))
    _L0_wmod = _w((lambda *s: np.random.randn(*s).astype(np.float32) * 0.05)(256, 6 * 256) * 256 ** (-0.5))
    _d = {'L0_attn_x': _L0_attn_in['x'], 'L0_attn_w_qkv': _L0_attn_in['w_qkv'], 'L0_attn_b_qkv': _L0_attn_in['b_qkv'], 'L0_attn_w_fc': _L0_attn_in['w_fc'], 'L0_attn_b_fc': _L0_attn_in['b_fc'], 'L0_attn_gamma': _L0_attn_in['gamma'], 'L0_attn_beta': _L0_attn_in['beta'], 'L0_ffn_W_r': _L0_ffn_in['W_r'], 'L0_ffn_W_k': _L0_ffn_in['W_k'], 'L0_ffn_W_v': _L0_ffn_in['W_v'], 'L0_ffn_mu_r': _L0_ffn_in['mu_r'], 'L0_ffn_mu_k': _L0_ffn_in['mu_k'], 'L0_c': _L0_c, 'L0_wmod': _L0_wmod}
    _x0 = _d['L0_attn_x']
    _d['L0_attn_x'] = jax.random.normal(jax.random.fold_in(jax.random.key(seed), 1), (8, 2048, 256), dtype=_x0.dtype)
    del _x0
    return _d

def reference(L0_attn_x, L0_attn_w_qkv, L0_attn_b_qkv, L0_attn_w_fc, L0_attn_b_fc, L0_attn_gamma, L0_attn_beta, L0_ffn_W_r, L0_ffn_W_k, L0_ffn_W_v, L0_ffn_mu_r, L0_ffn_mu_k, L0_c, L0_wmod):

    def _L0_attn_ref(x, w_qkv, b_qkv, w_fc, b_fc, gamma, beta):
        import jax, jax.numpy as jnp
        import numpy as np
        D_MODEL = 256
        N_HEAD = 8
        D_X = 64
        EPS = 1e-06
        B, L, D = x.shape
        H, dx = (N_HEAD, D_X)
        qkv = x @ w_qkv + b_qkv
        q, k, v = jnp.split(qkv, 3, axis=-1)
        q = q.reshape(B, L, H, dx).transpose(0, 2, 1, 3)
        k = k.reshape(B, L, H, dx).transpose(0, 2, 1, 3)
        v = v.reshape(B, L, H, dx).transpose(0, 2, 1, 3)
        scores = jnp.einsum('bhld,bhle->bhde', q, k) / jnp.sqrt(jnp.asarray(dx, x.dtype))
        attn = jax.nn.softmax(scores, axis=-1)
        out = jnp.einsum('bhld,bhde->bhle', v, attn)
        out = out.transpose(0, 2, 1, 3).reshape(B, L, H * dx)
        out = out @ w_fc + b_fc
        out = out + x
        mu = jnp.mean(out, axis=-1, keepdims=True)
        var = jnp.mean(jnp.square(out - mu), axis=-1, keepdims=True)
        out = (out - mu) * jax.lax.rsqrt(var + EPS) * gamma + beta
        return out

    def _L0_ffn_ref(x, W_r, W_k, W_v, mu_r, mu_k):
        import jax, jax.numpy as jnp
        import numpy as np
        DIM = 256

        def _reference_tuple_inner(x, W_r, W_k, W_v, mu_r, mu_k):
            B, T, C = x.shape
            x_prev = jnp.concatenate([jnp.zeros((B, 1, C), x.dtype), x[:, :-1, :]], axis=1)
            xr = mu_r * x + (1.0 - mu_r) * x_prev
            xk = mu_k * x + (1.0 - mu_k) * x_prev
            r = jax.nn.sigmoid(jnp.einsum('btc,dc->btd', xr, W_r))
            k = jnp.einsum('btc,dc->btd', xk, W_k)
            k_act = jnp.square(jax.nn.relu(k))
            out = r * jnp.einsum('btc,dc->btd', k_act, W_v)
            new_state = x[:, -1, :]
            return (out, new_state)
        return _reference_tuple_inner(x, W_r, W_k, W_v, mu_r, mu_k)[0]
    x = L0_attn_x
    mod = (_silu(L0_c) @ L0_wmod).reshape(L0_c.shape[0], 6, 1, -1)
    sa, ca, ga, sb, cb, gb = (mod[:, 0], mod[:, 1], mod[:, 2], mod[:, 3], mod[:, 4], mod[:, 5])
    ga = (2 * (ga >= 0) - 1) * jnp.maximum(jnp.abs(ga), 0.25)
    gb = (2 * (gb >= 0) - 1) * jnp.maximum(jnp.abs(gb), 0.25)
    h = _layernorm(x, axis=-1) * (1 + ca) + sa
    x = x + ga * _L0_attn_ref(h, L0_attn_w_qkv, L0_attn_b_qkv, L0_attn_w_fc, L0_attn_b_fc, L0_attn_gamma, L0_attn_beta)
    h = _layernorm(x, axis=-1) * (1 + cb) + sb
    x = x + gb * _L0_ffn_ref(h, L0_ffn_W_r, L0_ffn_W_k, L0_ffn_W_v, L0_ffn_mu_r, L0_ffn_mu_k)
    return x

_drawn_inputs = setup_inputs


def setup_inputs(seed=0):
    import zlib

    import numpy as np

    out = dict(_drawn_inputs(seed))
    spreads = {'L0_attn_gamma': (1.0, 0.2), 'L0_attn_beta': (0.0, 0.362)}
    factors = {'L0_attn_b_qkv': 5.515,
     'L0_attn_b_fc': 8.0,
     'L0_ffn_W_r': 8.0,
     'L0_ffn_W_k': 3.093,
     'L0_ffn_W_v': 2.83,
     'L0_ffn_mu_r': 8.0,
     'L0_ffn_mu_k': 5.086}
    for name, (base, spread) in spreads.items():
        noise = np.random.default_rng([zlib.crc32(name.encode()), seed]).standard_normal(out[name].shape)
        drawn = base * np.exp(spread * noise) if base else spread * noise
        out[name] = jnp.asarray(drawn.astype(out[name].dtype))
    for name, factor in factors.items():
        out[name] = (out[name] * factor).astype(out[name].dtype)
    return out
```

```python
from contextlib import ExitStack

import concourse.bass as bass
from concourse import mybir

F32 = mybir.dt.float32
ALU = mybir.AluOpType
ACT = mybir.ActivationFunctionType
AX = mybir.AxisListType.X

P = 128


def adaln_block(nc, x, w_qkv, b_qkv, w_fc, b_fc, gamma, beta, w_r, w_k, w_v, mu_r, mu_k, c, wmod, out):
    B, L, D = x.shape
    HD = w_fc.shape[0]
    DX = 64
    H = HD // DX
    KD = D // P
    NP = H // 2
    CT = 512
    CH = L // CT
    NT = CT // P
    LAST = D - 1
    QK = 2 * HD
    SM_SCALE = float(DX) ** -0.5
    EPS_LN, EPS_ATT = 1e-5, 1e-6
    assert (KD, NP, NT, CH) == (2, 4, 4, 4)

    x_v = x.rearrange("b (j t p) d -> b j p t d", p=P, t=NT)
    out_v = out.rearrange("b (j t p) d -> b j p t d", p=P, t=NT)

    with ExitStack() as ctx:
        def sb(name, shape):
            return ctx.enter_context(nc.sbuf_tensor(name, shape, F32))

        def bank(name):
            return ctx.enter_context(nc.psum_tensor(name, [P, 512], F32))

        def sem(name):
            return ctx.enter_context(nc.semaphore(name))

        gram = bank("gram")
        tr = [bank(f"tr{h}") for h in range(KD)]
        att = [bank(f"att{q}") for q in range(2)]
        work = [bank(f"work{w}") for w in range(3)]

        ident = sb("ident", [P, P])
        ident_c = sb("ident_c", [P, KD, D])
        last_c = sb("last_c", [P, D])
        neg_half, half, quarter, minus_one, eps_att = (
            sb(n, [P, NT]) for n in ("neg_half", "half", "quarter", "minus_one", "eps_att"))
        wqkv_sb = sb("wqkv_sb", [P, KD, 3 * HD])
        wqk_last = sb("wqk_last", [P, QK])
        bv_col = sb("bv_col", [P, NP])
        wfc_c = sb("wfc_c", [P, NP, D])
        w_ffn_t = sb("w_ffn_t", [P, 3, KD, D])
        mu_col = sb("mu_col", [P, 2, KD])
        wv_t = sb("wv_t", [P, NP, D])

        th_c = sb("th_c", [P, KD * B])
        silu_u = sb("silu_u", [P, KD * B])
        silu = sb("silu", [P, KD * B])
        mod_col = sb("mod_col", [P, 8, B])
        vb_col = sb("vb_col", [P, NP, B])
        col8 = sb("col8", [B, 2])
        fc_mean = sb("fc_mean", [P, NP])
        scratch = nc.dram_tensor("row_scratch", [B, 4 * D + QK + D], F32)

        rows = sb("rows", [P, 4, D])
        g_row = sb("g_row", [P, D])
        mod_now = sb("mod_now", [P, 4])
        wvf = sb("wvf", [P, KD, D])
        d_now = sb("d_now", [P, KD])
        neg_d = sb("neg_d", [P, 1])
        wqk_l = sb("wqk_l", [P, QK])
        wqk_aug = sb("wqk_aug", [P, KD, QK])
        wv_mod = sb("wv_mod", [P, NP, D])
        wv_aug = sb("wv_aug", [P, NP, D])
        res_d = sb("res_d", [P, KD, D])
        res = sb("res", [P, KD, D])
        g_sb = sb("g_sb", [P, KD, D])
        gq = sb("gq", [P, KD, HD])
        s_max = sb("s_max", [P, NP])
        s_dif = sb("s_dif", [P, NP, DX])
        s_exp = sb("s_exp", [P, NP, DX])
        s_sum = sb("s_sum", [P, NP])
        s_inv = sb("s_inv", [P, NP])
        attn = sb("attn", [P, NP, P])
        pv_t = sb("pv_t", [P, NP, D])
        m_sb = sb("m_sb", [P, KD, D])

        x_in = sb("x_in", [P, CH, NT, D])
        xb = sb("xb", [P, CH, NT, D])
        z = sb("z", [P, 2, NT, D])
        z_t = sb("z_t", [P, CH, KD, CT])
        st_a = sb("st_a", [P, CH, NT, 6])
        ag_a = sb("ag_a", [P, CH, 8, NT])
        sq_junk = ctx.enter_context(nc.sbuf_tensor("sq_junk", [P, NT, D], mybir.dt.bfloat16))
        ssq = sb("ssq", [P, 2, NT])
        ve_o = sb("ve_o", [P, 2, NT])
        rs_o = sb("rs_o", [P, 2, NT])
        t_buf = sb("t_buf", [P, NT, D])
        x2 = sb("x2", [P, CH, NT, D])
        st_2 = sb("st_2", [P, 2, NT, 6])
        ag_2 = sb("ag_2", [P, 2, 8, NT])
        z2 = sb("z2", [P, NT, D])
        h2t = sb("h2t", [P, KD, 1 + L])
        xk = sb("xk", [P, KD, CT])
        xr = sb("xr", [P, KD, CT])
        k_act = sb("k_act", [P, KD, CT])
        th_r = sb("th_r", [P, NT, D])
        y = sb("y", [P, 2, NT, D])

        dif = t_buf[:].rearrange("p t d -> p (t d)").rearrange("p (k n) -> p k n", k=KD)

        wmod_sb = x2[:, 0:3].rearrange("p j t d -> p (j t d)").rearrange("p (k n) -> p k n", k=KD)
        w_ffn = y[:].rearrange("p s t d -> p (s t d)")[:, 0:3 * KD * D].rearrange(
            "p (n k d) -> p n k d", n=3, k=KD)
        NR = 5 * D + QK
        room8 = xb[0:B].rearrange("p j t d -> p (j t d)")
        row8 = room8[:, 0:NR]
        tmp8 = room8[:, NR:NR + 4 * D].rearrange("p (n d) -> p n d", n=4)
        bqk8 = z2[0:B].rearrange("p t d -> p (t d)")
        c_sb, gamma8, beta8, bfc8 = (t_buf[0:B, n] for n in range(4))

        ident_ready = sem("ident_ready")
        const_ready = sem("const_ready")
        pool_step = sem("pool_step")
        c_loaded = sem("c_loaded")
        wmod_loaded = sem("wmod_loaded")
        wqkv_loaded = sem("wqkv_loaded")
        small_loaded = sem("small_loaded")
        wfc_loaded = sem("wfc_loaded")
        ffn_loaded = sem("ffn_loaded")
        c_turned = sem("c_turned")
        c_tanh = sem("c_tanh")
        silu_ready = sem("silu_ready")
        mod_done = sem("mod_done")
        mod_col_ready = sem("mod_col_ready")
        bias_done = sem("bias_done")
        row8_step = sem("row8_step")
        row8_ready = sem("row8_ready")
        vb_ready = sem("vb_ready")
        fc_step = sem("fc_step")
        fc_ready = sem("fc_ready")
        w_turned = sem("w_turned")
        w_copied = sem("w_copied")
        row8_stored = sem("row8_stored")
        rows_loaded = sem("rows_loaded")
        edge_loaded = sem("edge_loaded")
        now_ready = sem("now_ready")
        prep_step = sem("prep_step")
        qk_ready = sem("qk_ready")
        wv_step = sem("wv_step")
        wv_ready = sem("wv_ready")
        gram_done = sem("gram_done")
        g_up_ready = sem("g_up_ready")
        gram_turned = sem("gram_turned")
        g_ready = sem("g_ready")
        gq_done = sem("gq_done")
        gq_ready = sem("gq_ready")
        score_done = sem("score_done")
        sm_step = sem("sm_step")
        s_dif_ready = sem("s_dif_ready")
        exp_done = sem("exp_done")
        attn_ready = sem("attn_ready")
        pv_done = sem("pv_done")
        pv_ready = sem("pv_ready")
        m_done = sem("m_done")
        m_ready = sem("m_ready")
        x_loaded = [sem(f"x_loaded{j}") for j in range(CH)]
        st_a_done = sem("st_a_done")
        ag_a_step = sem("ag_a_step")
        rs_a_ready = sem("rs_a_ready")
        z_ready = sem("z_ready")
        z_turned = sem("z_turned")
        z_t_ready = sem("z_t_ready")
        xb_ready = sem("xb_ready")
        att_done = sem("att_done")
        ssq_ready = sem("ssq_ready")
        ve_o_done = sem("ve_o_done")
        rs_o_ready = sem("rs_o_ready")
        t_done = sem("t_done")
        x2_ready = sem("x2_ready")
        st_2_done = sem("st_2_done")
        ag_2_step = sem("ag_2_step")
        rs_2_step = sem("rs_2_step")
        rs_2_ready = sem("rs_2_ready")
        z2_ready = sem("z2_ready")
        z2_turned = sem("z2_turned")
        h2_ready = sem("h2_ready")
        dif_done = sem("dif_done")
        xk_ready = sem("xk_ready")
        xr_ready = sem("xr_ready")
        k_done = sem("k_done")
        k_pos_ready = sem("k_pos_ready")
        k_act_ready = sem("k_act_ready")
        r_done = sem("r_done")
        th_ready = sem("th_ready")
        o_done = sem("o_done")
        ro_ready = sem("ro_ready")
        y_ready = sem("y_ready")
        y_stored = [sem(f"y_stored{s}") for s in range(2)]

        def wait_past(eng, semaphore, count):
            if not isinstance(count, int) or count > 0:
                eng.wait_ge(semaphore, count)

        block = ctx.enter_context(nc.Block())

        @block.sync
        def _(sp):
            def load_x(b, j):
                sp.dma_start(x_in[:, j], x_v[b, j]).then_inc(x_loaded[j], 16)

            def load_rows(b):
                src = scratch[b, 0:4 * D].partition_broadcast(P)
                sp.dma_start(rows[:].rearrange("p r d -> p (r d)"), src).then_inc(rows_loaded, 16)
                sp.dma_start(wqk_aug[P - 1:P, KD - 1, :], scratch[b, 4 * D:4 * D + QK].unsqueeze(0)).then_inc(edge_loaded, 16)
                sp.dma_start(res[P - 1:P, KD - 1, :], scratch[b, 4 * D + QK:5 * D + QK].unsqueeze(0)).then_inc(edge_loaded, 16)

            def next_x(b, j):
                sp.wait_ge(z_ready, CH * (b - 1) + j + 1)
                sp.wait_ge(xb_ready, CH * (b - 1) + j + 1)
                load_x(b, j)

            def next_rows(b):
                sp.wait_ge(xb_ready, CH * b)
                sp.wait_ge(now_ready, b)
                sp.wait_ge(m_ready, b)
                load_rows(b)

            def store_y(b, j):
                sp.wait_ge(y_ready, CH * b + j + 1)
                sp.dma_start(out_v[b, j], y[:, j % 2]).then_inc(y_stored[j % 2], 16)

            def row_steps(b):
                next_rows(b + 1)
                next_x(b + 2, 0)
                next_x(b + 2, 1)
                store_y(b, 0)
                next_x(b + 2, 2)
                next_x(b + 2, 3)
                for j in range(1, CH):
                    store_y(b, j)

            sp.dma_start(c_sb, c).then_inc(c_loaded, 16)
            sp.dma_start(wmod_sb, wmod.rearrange("(k p) n -> p k n", p=P)).then_inc(wmod_loaded, 16)
            for j in range(CH):
                load_x(0, j)
            sp.dma_start(w_ffn[:, 0], w_r.rearrange("(k p) n -> p k n", p=P)).then_inc(ffn_loaded, 16)
            sp.dma_start(w_ffn[:, 1], w_k.rearrange("(k p) n -> p k n", p=P)).then_inc(ffn_loaded, 16)
            sp.dma_start(w_ffn[:, 2], w_v.rearrange("(k p) n -> p k n", p=P)).then_inc(ffn_loaded, 16)
            sp.wait_ge(row8_ready, 1)
            sp.dma_start(scratch[:, :], row8).then_inc(row8_stored, 16)
            sp.wait_ge(row8_stored, 16)
            load_rows(0)
            for j in range(CH):
                next_x(1, j)
            row_steps(0)
            with sp.Fori(1, B - 2) as b:
                row_steps(b)
            next_rows(B - 1)
            for b in (B - 2, B - 1):
                for j in range(CH):
                    store_y(b, j)
            for s in range(2):
                sp.wait_ge(y_stored[s], 16 * B * CH // 2)

        @block.gpsimd
        def _(pool):
            def build_constants():
                nc.gpsimd.memset(ident[:], 0.0).then_inc(pool_step, 1)
                nc.gpsimd.memset(ident_c[:], -1.0 / D).then_inc(pool_step, 1)
                nc.gpsimd.memset(last_c[:], -1.0 / D).then_inc(pool_step, 1)
                pool.wait_ge(pool_step, 3)
                nc.gpsimd.affine_select(out=ident[:], in_=ident[:], compare_op=ALU.not_equal, fill=1.0, base=0,
                                        pattern=[[-1, P]], channel_multiplier=1).then_inc(ident_ready, 1)
                nc.gpsimd.affine_select(out=ident_c[:], in_=ident_c[:], compare_op=ALU.not_equal, fill=1.0 - 1.0 / D,
                                        base=0, pattern=[[P, KD], [-1, D]], channel_multiplier=1).then_inc(const_ready, 1)
                nc.gpsimd.memset(last_c[:, LAST:D], 1.0 - 1.0 / D).then_inc(const_ready, 1)
                nc.gpsimd.memset(half[:], 0.5).then_inc(const_ready, 1)
                nc.gpsimd.memset(minus_one[:], -1.0).then_inc(const_ready, 1)
                nc.gpsimd.memset(quarter[:], 0.25).then_inc(const_ready, 1)
                nc.gpsimd.memset(eps_att[:], EPS_ATT).then_inc(const_ready, 1)
                nc.gpsimd.memset(neg_half[:], -0.5).then_inc(const_ready, 1)
                nc.gpsimd.memset(attn[:], 0.0).then_inc(const_ready, 1)
                nc.gpsimd.memset(h2t[:, :, 0:1], 0.0).then_inc(const_ready, 1)
                nc.gpsimd.memset(z[:, :, :, LAST:D], 1.0).then_inc(const_ready, 1)
                pool.wait_ge(const_ready, 10)

            def layernorm_factors(i, st, ag, st_done, ag_step, ready, eps):
                pool.wait_ge(st_done, i + 1)
                nc.gpsimd.tensor_tensor(ag[:, 0], st[:, :, 1], st[:, :, 4], ALU.add)
                nc.gpsimd.tensor_tensor(ag[:, 1], st[:, :, 1], st[:, :, 4], ALU.subtract)
                nc.gpsimd.tensor_tensor(ag[:, 2], st[:, :, 2], st[:, :, 5], ALU.add).then_inc(ag_step, 1)
                pool.wait_ge(ag_step, 4 * i + 1)
                nc.gpsimd.tensor_tensor(ag[:, 3], ag[:, 0], half[:], ALU.mult)
                nc.gpsimd.tensor_tensor(ag[:, 4], ag[:, 1], ag[:, 1], ALU.mult)
                nc.gpsimd.tensor_scalar(ag[:, 5], ag[:, 2], 1.0 / D, eps, ALU.mult, ALU.add).then_inc(ag_step, 1)
                pool.wait_ge(ag_step, 4 * i + 2)
                nc.gpsimd.tensor_tensor(ag[:, 4], ag[:, 4], quarter[:], ALU.mult).then_inc(ag_step, 1)
                pool.wait_ge(ag_step, 4 * i + 3)
                nc.gpsimd.tensor_tensor(ag[:, 6], ag[:, 4], ag[:, 5], ALU.add).then_inc(ag_step, 1)
                pool.wait_ge(ag_step, 4 * i + 4)
                nc.gpsimd.tensor_tensor(ag[:, 7], ag[:, 6], neg_half[:], ALU.pow).then_inc(ready, 1)

            def rstd_a(b, j):
                layernorm_factors(CH * b + j, st_a[:, j], ag_a[:, j], st_a_done, ag_a_step, rs_a_ready, EPS_LN)

            def rstd_2(b, j):
                i, ag = CH * b + j, ag_2[:, j % 2]
                layernorm_factors(i, st_2[:, j % 2], ag, st_2_done, ag_2_step, rs_2_step, EPS_LN)
                nc.gpsimd.tensor_tensor(ag[:, 0], ag[:, 3], minus_one[:], ALU.mult).then_inc(rs_2_step, 1)
                pool.wait_ge(rs_2_step, 2 * i + 2)
                nc.gpsimd.tensor_tensor(ag[:, 1], ag[:, 0], ag[:, 7], ALU.mult).then_inc(rs_2_ready, 1)

            def rstd_o(b, j):
                i, s = CH * b + j, j % 2
                pool.wait_ge(ssq_ready, i + 1)
                nc.gpsimd.tensor_tensor(ve_o[:, s], ssq[:, s], eps_att[:], ALU.add).then_inc(ve_o_done, 1)
                pool.wait_ge(ve_o_done, i + 1)
                nc.gpsimd.tensor_tensor(rs_o[:, s], ve_o[:, s], neg_half[:], ALU.pow).then_inc(rs_o_ready, 1)

            def make_xb(b, j, first=False):
                pool.wait_ge(x_loaded[j], 16 * (b + 1))
                pool.wait_ge(rows_loaded, 16 * (b + 1))
                if not first:
                    pool.wait_ge(x2_ready, CH * (b - 1) + j + 1)
                nc.gpsimd.tensor_tensor(xb[:, j], x_in[:, j], rows[:, 2].unsqueeze(1).to_broadcast([P, NT, D]),
                                        ALU.add).then_inc(xb_ready, 1)

            def prep_wv(b):
                pool.wait_ge(rows_loaded, 16 * (b + 1))
                wait_past(pool, m_ready, b)
                nc.gpsimd.tensor_tensor(wv_mod[:], wv_t[:], rows[:, 0].unsqueeze(1).to_broadcast([P, NP, D]),
                                        ALU.mult).then_inc(wv_step, 1)
                pool.wait_ge(wv_step, b + 1)
                nc.gpsimd.tensor_tensor(wv_aug[:, :, 0:LAST], wv_mod[:, :, 0:LAST],
                                        wv_mod[:, :, LAST:D].to_broadcast([P, NP, LAST]), ALU.subtract)
                nc.gpsimd.tensor_copy(wv_aug[:, :, LAST], vb_col[:, :, b]).then_inc(wv_ready, 1)

            def add_y(b, j):
                i, s = CH * b + j, j % 2
                pool.wait_ge(ro_ready, 2 * i + 2)
                nc.gpsimd.tensor_tensor(y[:, s], y[:, s], x2[:, j], ALU.add).then_inc(y_ready, 1)

            def row_steps(b, last):
                n = b + 1
                for j in range(CH):
                    if not last and j == 0:
                        rstd_a(n, 0)
                        rstd_a(n, 1)
                    if j > 1:
                        add_y(b, j - 2)
                    rstd_o(b, j)
                    rstd_2(b, j)
                    if not last:
                        if j + 2 < CH:
                            rstd_a(n, j + 2)
                        make_xb(n, j)
                        if j == 1:
                            prep_wv(n)
                add_y(b, CH - 2)
                add_y(b, CH - 1)

            build_constants()
            for j in range(CH):
                rstd_a(0, j)
            pool.wait_ge(w_copied, 5)
            pool.wait_ge(vb_ready, 1)
            prep_wv(0)
            for j in range(CH):
                make_xb(0, j, first=True)
            row_steps(0, False)
            with pool.Fori(1, B - 1) as b:
                row_steps(b, False)
            row_steps(B - 1, True)

        @block.scalar
        def _(act):
            def load_weights():
                act.dma_start(wqkv_sb[:], w_qkv.rearrange("(k p) n -> p k n", p=P)).then_inc(wqkv_loaded, 16)
                act.dma_start(bqk8, b_qkv[0:QK].partition_broadcast(B)).then_inc(small_loaded, 16)
                act.dma_start(gamma8, gamma.partition_broadcast(B)).then_inc(small_loaded, 16)
                act.dma_start(beta8, beta.partition_broadcast(B)).then_inc(small_loaded, 16)
                act.dma_start(bfc8, b_fc.partition_broadcast(B)).then_inc(small_loaded, 16)
                act.dma_start(wqk_last[:], w_qkv[LAST, 0:QK].partition_broadcast(P)).then_inc(small_loaded, 16)
                with nc.allow_non_contiguous_dma(reason="three short vectors onto partitions"):
                    act.dma_start(bv_col[:], b_qkv[QK:3 * HD].rearrange("(n p) -> p n", p=P)).then_inc(small_loaded, 16)
                    act.dma_start(mu_col[:, 0], mu_r.rearrange("(k p) -> p k", p=P)).then_inc(small_loaded, 16)
                    act.dma_start(mu_col[:, 1], mu_k.rearrange("(k p) -> p k", p=P)).then_inc(small_loaded, 16)
                act.dma_start(wfc_c[:], w_fc.rearrange("(n p) d -> p n d", p=P)).then_inc(wfc_loaded, 16)

            def setup():
                act.wait_ge(c_turned, 1)
                nc.scalar.activation(th_c[:], work[0][:, 0:KD * B], ACT.Tanh, scale=0.5).then_inc(c_tanh, 1)
                for n, (dst, src) in enumerate([
                        (wv_t[:, 0:2], gram), (wv_t[:, 2:4], att[0]),
                        (w_ffn_t[:, 0], work[0]), (w_ffn_t[:, 1], work[1]), (w_ffn_t[:, 2], work[2])]):
                    act.wait_ge(w_turned, n + 1)
                    nc.scalar.activation(dst.rearrange("p a d -> p (a d)"), src[:], ACT.Copy).then_inc(w_copied, 1)

            def copy_z_t(b, j):
                i = CH * b + j
                for h in range(KD):
                    act.wait_ge(z_turned, 2 * i + h + 1)
                    nc.scalar.activation(z_t[:, j, h], tr[h][:], ACT.Copy).then_inc(z_t_ready, 1)

            def copy_gram(b):
                act.wait_ge(gram_done, b + 1)
                nc.scalar.activation(g_sb[:, 0], gram[:, 0:D], ACT.Copy)
                nc.scalar.activation(g_sb[:, 1, P:D], gram[:, D:D + P], ACT.Copy).then_inc(g_up_ready, 1)

            def copy_gram_low(b):
                act.wait_ge(gram_turned, b + 1)
                nc.scalar.activation(g_sb[:, 1, 0:P], gram[:, D + P:2 * D], ACT.Copy).then_inc(g_ready, 1)

            def copy_gq(b):
                for m in range(KD):
                    act.wait_ge(gq_done, 2 * b + m + 1)
                    nc.scalar.activation(gq[:, m], att[m][:], ACT.Copy).then_inc(gq_ready, 1)

            def exps(b):
                act.wait_ge(s_dif_ready, b + 1)
                nc.scalar.activation(s_exp[:], s_dif[:], ACT.Exp, scale=SM_SCALE).then_inc(exp_done, 1)

            def copy_pv(b):
                for g in range(2):
                    act.wait_ge(pv_done, 2 * b + g + 1)
                    nc.scalar.activation(pv_t[:, 2 * g:2 * g + 2].rearrange("p n d -> p (n d)"), att[g][:],
                                         ACT.Copy).then_inc(pv_ready, 1)

            def squares(b, j):
                i, s = CH * b + j, j % 2
                for t in range(NT):
                    if t % 2 == 0:
                        act.wait_ge(att_done, 2 * i + t // 2 + 1)
                    sq = nc.scalar.activation(sq_junk[:, t], att[t // 2][:, (t % 2) * D:(t % 2 + 1) * D], ACT.Square,
                                              scale=float(D) ** -0.5, accum_out=ssq[:, s, t:t + 1])
                sq.then_inc(ssq_ready, 1)

            def copy_h2(b, j):
                i = CH * b + j
                for h in range(KD):
                    act.wait_ge(z2_turned, 2 * i + h + 1)
                    nc.scalar.activation(h2t[:, h, 1 + j * CT:1 + (j + 1) * CT], tr[h][:], ACT.Identity,
                                         bias=mod_now[:, h:h + 1], scale=mod_now[:, 2 + h:3 + h]).then_inc(h2_ready, 1)

            def k_and_r(b, j):
                i = CH * b + j
                for h in range(KD):
                    act.wait_ge(k_done, 2 * i + h + 1)
                    nc.scalar.activation(k_act[:, h], work[h][:], ACT.Relu).then_inc(k_pos_ready, 1)
                act.wait_ge(k_pos_ready, 2 * i + 2)
                nc.scalar.activation(k_act[:], k_act[:], ACT.Square).then_inc(k_act_ready, 1)
                for q in range(2):
                    act.wait_ge(r_done, 2 * i + q + 1)
                    nc.scalar.activation(th_r[:, 2 * q:2 * q + 2].rearrange("p t d -> p (t d)"), work[2 - 2 * q][:],
                                         ACT.Tanh, scale=0.5).then_inc(th_ready, 1)

            def make_z2(b, j):
                i, s = CH * b + j, j % 2
                act.wait_ge(rs_2_ready, i + 1)
                for t in range(NT):
                    ins = nc.scalar.activation(z2[:, t], x2[:, j, t], ACT.Identity, bias=ag_2[:, s, 1, t:t + 1],
                                               scale=ag_2[:, s, 7, t:t + 1])
                ins.then_inc(z2_ready, 1)

            def row_steps(b, last):
                n = b + 1
                for j in range(CH):
                    squares(b, j)
                    if j:
                        copy_h2(b, j - 1)
                    if not last:
                        copy_z_t(n, j)
                        if j == CH - 1:
                            copy_gram(n)
                    if j:
                        k_and_r(b, j - 1)
                    if not last and j == CH - 1:
                        copy_gram_low(n)
                    make_z2(b, j)
                copy_h2(b, CH - 1)
                if not last:
                    copy_gq(n)
                    exps(n)
                k_and_r(b, CH - 1)
                if not last:
                    copy_pv(n)

            load_weights()
            setup()
            for j in range(CH):
                copy_z_t(0, j)
            copy_gram(0)
            copy_gram_low(0)
            copy_gq(0)
            exps(0)
            copy_pv(0)
            row_steps(0, False)
            with act.Fori(1, B - 1) as b:
                row_steps(b, False)
            row_steps(B - 1, True)

        @block.vector
        def _(dve):
            def setup():
                dve.wait_ge(c_tanh, 1)
                nc.vector.scalar_tensor_tensor(silu_u[:], th_c[:], 1.0, work[0][:, 0:KD * B], ALU.add,
                                               ALU.mult).then_inc(row8_step, 1)
                dve.wait_ge(row8_step, 1)
                nc.vector.tensor_scalar(silu[:], silu_u[:], 0.5, None, ALU.mult).then_inc(silu_ready, 1)
                dve.wait_ge(mod_done, 1)
                flat = mod_col[:].rearrange("p m b -> p (m b)")
                w = KD * B
                for m, add in enumerate((0.0, 1.0, 0.0, 1.0)):
                    ins = nc.vector.tensor_scalar(flat[:, m * w:(m + 1) * w], att[0][:, m * w:(m + 1) * w], add, None, ALU.add)
                ins.then_inc(mod_col_ready, 1)
                dve.wait_ge(small_loaded, 16 * 8)
                nc.vector.tensor_scalar(row8[:, 0:D], work[0][0:B, D:2 * D], 1.0, None, ALU.add)
                steps = 1
                for n, src in enumerate((work[1][0:B, 0:D], work[2][0:B, D:2 * D])):
                    size, sign = tmp8[:, 2 * n], tmp8[:, 2 * n + 1]
                    nc.vector.tensor_scalar(sign, src, -1.0, None, ALU.mult).then_inc(row8_step, 1)
                    dve.wait_ge(row8_step, steps + 1)
                    nc.vector.tensor_tensor(size, sign, src, ALU.max).then_inc(row8_step, 1)
                    dve.wait_ge(row8_step, steps + 2)
                    nc.vector.tensor_scalar(sign, src, 0.0, 2.0, ALU.is_ge, ALU.mult).then_inc(row8_step, 1)
                    nc.vector.tensor_scalar(size, size, 0.25, None, ALU.max).then_inc(row8_step, 1)
                    dve.wait_ge(row8_step, steps + 4)
                    nc.vector.scalar_tensor_tensor(size, sign, -1.0, size, ALU.add, ALU.mult).then_inc(row8_step, 1)
                    dve.wait_ge(row8_step, steps + 5)
                    steps += 5
                nc.vector.tensor_tensor(row8[:, D:2 * D], tmp8[:, 0], gamma8, ALU.mult)
                nc.vector.tensor_tensor(row8[:, 2 * D:3 * D], tmp8[:, 0], beta8, ALU.mult)
                nc.vector.tensor_scalar(row8[:, 3 * D:4 * D], tmp8[:, 2], 0.5, None, ALU.mult)
                e = 4 * D + QK
                nc.vector.scalar_tensor_tensor(row8[:, e:e + D], work[0][0:B, 0:D], 0.0, bfc8, ALU.add, ALU.add,
                                               accum_out=col8[:, 0:1]).then_inc(row8_step, 1)
                dve.wait_ge(row8_step, steps + 1)
                nc.vector.tensor_scalar(col8[:, 1:2], col8[:, 0:1], 1.0 / D, None, ALU.mult).then_inc(row8_step, 1)
                dve.wait_ge(row8_step, steps + 2)
                nc.vector.tensor_scalar(row8[:, e:e + D], row8[:, e:e + D], col8[:, 1:2], None,
                                        ALU.subtract).then_inc(row8_step, 1)
                dve.wait_ge(bias_done, 1)
                for g in range(2):
                    ins = nc.vector.tensor_tensor(row8[:, 4 * D + g * HD:4 * D + (g + 1) * HD], tr[g][0:B, :],
                                                  bqk8[:, g * HD:(g + 1) * HD], ALU.add)
                ins.then_inc(row8_ready, 1)
                for p in range(NP):
                    ins = nc.vector.tensor_scalar(vb_col[:, p], att[1][:, p * B:(p + 1) * B], bv_col[:, p:p + 1], None, ALU.add)
                ins.then_inc(vb_ready, 1)
                dve.wait_ge(wfc_loaded, 16)
                nc.vector.tensor_reduce(fc_mean[:], wfc_c[:], AX, ALU.add).then_inc(fc_step, 1)
                dve.wait_ge(fc_step, 1)
                nc.vector.tensor_scalar(fc_mean[:], fc_mean[:], 1.0 / D, None, ALU.mult).then_inc(fc_step, 1)
                dve.wait_ge(fc_step, 2)
                for p in range(NP):
                    ins = nc.vector.tensor_scalar(wfc_c[:, p], wfc_c[:, p], fc_mean[:, p:p + 1], None, ALU.subtract)
                ins.then_inc(fc_ready, 1)

            def stats_a(b, j):
                i = CH * b + j
                dve.wait_ge(x_loaded[j], 16 * (b + 1))
                for t in range(NT):
                    ins = nc.vector.bn_stats(st_a[:, j, t], x_in[:, j, t])
                ins.then_inc(st_a_done, 1)

            def make_z(b, j, first=False):
                i = CH * b + j
                dve.wait_ge(rs_a_ready, i + 1)
                if not (first and j < 2):
                    dve.wait_ge(z_turned, 2 * (i - 2) + 2)
                for t in range(NT):
                    ins = nc.vector.tensor_scalar(z[:, j % 2, t, 0:LAST], x_in[:, j, t, 0:LAST], ag_a[:, j, 3, t:t + 1],
                                                  ag_a[:, j, 7, t:t + 1], ALU.subtract, ALU.mult)
                ins.then_inc(z_ready, 1)

            def make_x2(b, j):
                i, s = CH * b + j, j % 2
                wait_past(dve, xr_ready, i)
                dve.wait_ge(rs_o_ready, i + 1)
                for t in range(NT):
                    ins = nc.vector.scalar_tensor_tensor(t_buf[:, t], att[t // 2][:, (t % 2) * D:(t % 2 + 1) * D],
                                                         rs_o[:, s, t:t + 1], g_row[:], ALU.mult, ALU.mult)
                ins.then_inc(t_done, 1)
                dve.wait_ge(t_done, i + 1)
                dve.wait_ge(xb_ready, i + 1)
                nc.vector.tensor_tensor(x2[:, j], t_buf[:], xb[:, j], ALU.add).then_inc(x2_ready, 1)

            def stats_2(b, j):
                i, s = CH * b + j, j % 2
                dve.wait_ge(x2_ready, i + 1)
                for t in range(NT):
                    ins = nc.vector.bn_stats(st_2[:, s, t], x2[:, j, t])
                ins.then_inc(st_2_done, 1)

            def mix(b, j):
                i = CH * b + j
                dve.wait_ge(h2_ready, 2 * i + 2)
                prev = h2t[:, :, j * CT:(j + 1) * CT]
                nc.vector.tensor_tensor(dif, h2t[:, :, 1 + j * CT:1 + (j + 1) * CT], prev, ALU.subtract).then_inc(dif_done, 1)
                dve.wait_ge(dif_done, i + 1)
                for n, (dst, ready) in enumerate(((xk, xk_ready), (xr, xr_ready))):
                    for h in range(KD):
                        ins = nc.vector.scalar_tensor_tensor(dst[:, h], dif[:, h], mu_col[:, 1 - n, h:h + 1], prev[:, h],
                                                             ALU.mult, ALU.add)
                    ins.then_inc(ready, 1)

            def gate_o(b, j):
                i, s = CH * b + j, j % 2
                wait_past(dve, y_stored[s], 16 * (2 * b + j // 2))
                dve.wait_ge(th_ready, 2 * i + 2)
                for q in range(2):
                    dve.wait_ge(o_done, 2 * i + q + 1)
                    nc.vector.scalar_tensor_tensor(y[:, s, 2 * q:2 * q + 2].rearrange("p t d -> p (t d)"),
                                                   th_r[:, 2 * q:2 * q + 2].rearrange("p t d -> p (t d)"), 1.0,
                                                   work[1 + q][:], ALU.add, ALU.mult).then_inc(ro_ready, 1)

            def take_rows(b):
                nc.vector.tensor_copy(g_row[:], rows[:, 1])
                nc.vector.tensor_copy(mod_now[:], mod_col[:, 4:8, b])
                nc.vector.tensor_tensor(wvf[:], w_ffn_t[:, 2], rows[:, 3].unsqueeze(1).to_broadcast([P, KD, D]),
                                        ALU.mult).then_inc(now_ready, 1)
                dve.wait_ge(now_ready, b + 1)

            def prep_qk(b):
                dve.wait_ge(rows_loaded, 16 * (b + 1))
                nc.vector.tensor_scalar(neg_d[:], rows[:, 0, LAST:D], -1.0, None, ALU.mult).then_inc(prep_step, 1)
                nc.vector.tensor_copy(d_now[:], mod_col[:, 2:4, b]).then_inc(prep_step, 1)
                dve.wait_ge(prep_step, 4 * b + 2)
                nc.vector.tensor_scalar(wqk_l[:], wqk_last[:], neg_d[:], None, ALU.mult).then_inc(prep_step, 1)
                for k in range(KD):
                    ins = nc.vector.tensor_scalar(res_d[:, k], ident_c[:, k], d_now[:, k:k + 1], None, ALU.mult)
                ins.then_inc(prep_step, 1)
                dve.wait_ge(prep_step, 4 * b + 4)
                for k in range(KD):
                    n = P if k < KD - 1 else P - 1
                    nc.vector.scalar_tensor_tensor(wqk_aug[0:n, k], wqkv_sb[0:n, k, 0:QK], d_now[0:n, k:k + 1],
                                                   wqk_l[0:n], ALU.mult, ALU.add)
                    ins = nc.vector.scalar_tensor_tensor(res[0:n, k], last_c[0:n], neg_d[0:n], res_d[0:n, k],
                                                         ALU.mult, ALU.add)
                ins.then_inc(qk_ready, 1)

            def softmax_dif(b):
                dve.wait_ge(score_done, b + 1)
                for g in range(2):
                    lo = g * DX
                    block = gram[lo:lo + DX, :].rearrange("p (n e) -> p n e", n=NP)[:, :, lo:lo + DX]
                    nc.vector.tensor_reduce(s_max[lo:lo + DX], block, AX, ALU.max).then_inc(sm_step, 1)
                dve.wait_ge(sm_step, 4 * b + 2)
                for g in range(2):
                    lo = g * DX
                    block = gram[lo:lo + DX, :].rearrange("p (n e) -> p n e", n=NP)[:, :, lo:lo + DX]
                    ins = nc.vector.tensor_tensor(s_dif[lo:lo + DX], block,
                                                  s_max[lo:lo + DX].unsqueeze(2).to_broadcast([DX, NP, DX]), ALU.subtract)
                ins.then_inc(s_dif_ready, 1)

            def softmax_norm(b):
                dve.wait_ge(exp_done, b + 1)
                nc.vector.tensor_reduce(s_sum[:], s_exp[:], AX, ALU.add).then_inc(sm_step, 1)
                dve.wait_ge(sm_step, 4 * b + 3)
                nc.vector.reciprocal(s_inv[:], s_sum[:]).then_inc(sm_step, 1)
                dve.wait_ge(sm_step, 4 * b + 4)
                for g in range(2):
                    lo = g * DX
                    ins = nc.vector.tensor_tensor(attn[lo:lo + DX, :, lo:lo + DX], s_exp[lo:lo + DX],
                                                  s_inv[lo:lo + DX].unsqueeze(2).to_broadcast([DX, NP, DX]), ALU.mult)
                ins.then_inc(attn_ready, 1)

            def make_m(b):
                dve.wait_ge(m_done, b + 1)
                dve.wait_ge(edge_loaded, 32 * (b + 1))
                nc.vector.tensor_tensor(m_sb[:].rearrange("p k d -> p (k d)"), gram[:],
                                        res[:].rearrange("p k d -> p (k d)"), ALU.add).then_inc(m_ready, 1)

            def row_steps(b, last):
                n = b + 1
                for j in range(CH):
                    if j > 1:
                        gate_o(b, j - 2)
                    if not last:
                        if j == 0:
                            stats_a(n, 0)
                            stats_a(n, 1)
                        elif j + 1 < CH:
                            stats_a(n, j + 1)
                    if j == 0:
                        take_rows(b)
                    if not last:
                        if j == 0:
                            make_z(n, 0)
                        if j + 1 < CH and j:
                            make_z(n, j + 1)
                    if j:
                        mix(b, j - 1)
                    make_x2(b, j)
                    stats_2(b, j)
                    if not last and j == 0:
                        make_z(n, 1)
                        prep_qk(n)
                gate_o(b, CH - 2)
                mix(b, CH - 1)
                if not last:
                    softmax_dif(n)
                    softmax_norm(n)
                gate_o(b, CH - 1)
                if not last:
                    make_m(n)

            setup()
            dve.wait_ge(const_ready, 10)
            dve.wait_ge(wqkv_loaded, 16)
            dve.wait_ge(w_copied, 5)
            stats_a(0, 0)
            stats_a(0, 1)
            make_z(0, 0, first=True)
            stats_a(0, 2)
            make_z(0, 1, first=True)
            stats_a(0, 3)
            prep_qk(0)
            make_z(0, 2, first=True)
            make_z(0, 3, first=True)
            softmax_dif(0)
            softmax_norm(0)
            make_m(0)
            row_steps(0, False)
            with dve.Fori(1, B - 1) as b:
                row_steps(b, False)
            row_steps(B - 1, True)

        @block.tensor
        def _(pe):
            mm = nc.tensor.matmul

            def setup():
                pe.wait_ge(ident_ready, 1)
                pe.wait_ge(c_loaded, 16)
                for k in range(KD):
                    ins = nc.tensor.transpose(work[0][:, k * B:(k + 1) * B], c_sb[:, k * P:(k + 1) * P], ident[0:B, 0:B])
                ins.then_inc(c_turned, 1)
                pe.wait_ge(silu_ready, 1)
                pe.wait_ge(wmod_loaded, 16)
                for n in range(3):
                    for k in range(KD):
                        mm(work[n][0:B, :], silu[:, k * B:(k + 1) * B], wmod_sb[:, k, n * 512:(n + 1) * 512],
                           start=(k == 0), stop=(k == KD - 1))
                for n, m in enumerate((0, 1, 2, 3, 6, 7, 8, 9)):
                    for k in range(KD):
                        ins = mm(att[0][:, n * B:(n + 1) * B], wmod_sb[:, k, m * P:(m + 1) * P], silu[:, k * B:(k + 1) * B],
                                 start=(k == 0), stop=(k == KD - 1))
                ins.then_inc(mod_done, 1)
                pe.wait_ge(mod_col_ready, 1)
                pe.wait_ge(wqkv_loaded, 16)
                for g in range(2):
                    for k in range(KD):
                        mm(tr[g][0:B, :], mod_col[:, k, :], wqkv_sb[:, k, g * HD:(g + 1) * HD],
                           start=(k == 0), stop=(k == KD - 1))
                for p in range(NP):
                    for k in range(KD):
                        ins = mm(att[1][:, p * B:(p + 1) * B], wqkv_sb[:, k, QK + p * P:QK + (p + 1) * P], mod_col[:, k, :],
                                 start=(k == 0), stop=(k == KD - 1))
                ins.then_inc(bias_done, 1)
                for g, dst in enumerate((gram, att[0])):
                    for n in range(2):
                        p = 2 * g + n
                        for k in range(KD):
                            ins = nc.tensor.transpose(dst[:, n * D + k * P:n * D + (k + 1) * P],
                                                      wqkv_sb[:, k, QK + p * P:QK + (p + 1) * P], ident[:])
                    ins.then_inc(w_turned, 1)
                pe.wait_ge(ffn_loaded, 48)
                pe.wait_ge(row8_ready, 1)
                for n in range(3):
                    for ch in range(KD):
                        for dh in range(KD):
                            ins = nc.tensor.transpose(work[n][:, ch * D + dh * P:ch * D + (dh + 1) * P],
                                                      w_ffn[:, n, dh, ch * P:(ch + 1) * P], ident[:])
                    ins.then_inc(w_turned, 1)

            def gram_and_turn(b, j, first=False):
                i = CH * b + j
                pe.wait_ge(z_ready, i + 1)
                if j == 0 and not first:
                    pe.wait_ge(m_ready, b)
                for t in range(NT):
                    for k in range(KD):
                        ins = mm(gram[:, k * D:(k + 1) * D - k * P], z[:, j % 2, t, k * P:(k + 1) * P], z[:, j % 2, t, k * P:D],
                                 start=(j == 0 and t == 0 and k == 0), stop=(j == CH - 1 and t == NT - 1),
                                 skip_group_check=True)
                if j == CH - 1:
                    ins.then_inc(gram_done, 1)
                if first:
                    if j:
                        pe.wait_ge(z_t_ready, 2 * j)
                else:
                    wait_past(pe, h2_ready, 2 * (CH * (b - 1) + j))
                for h in range(KD):
                    for t in range(NT):
                        ins = nc.tensor.transpose(tr[h][:, t * P:(t + 1) * P], z[:, j % 2, t, h * P:(h + 1) * P], ident[:])
                    ins.then_inc(z_turned, 1)

            def attention(b, j):
                i = CH * b + j
                pe.wait_ge(m_ready, b + 1)
                pe.wait_ge(z_t_ready, 2 * i + 2)
                wait_past(pe, t_done, i)
                for q in range(2):
                    for t in (2 * q, 2 * q + 1):
                        for k in range(KD):
                            ins = mm(att[q][:, (t % 2) * D:(t % 2 + 1) * D], z_t[:, j, k, t * P:(t + 1) * P], m_sb[:, k],
                                     start=(k == 0), stop=(k == KD - 1))
                    ins.then_inc(att_done, 1)

            def turn_z2(b, j, last):
                i = CH * b + j
                pe.wait_ge(z2_ready, i + 1)
                if not last:
                    pe.wait_ge(z_t_ready, 2 * (i + CH) + 2)
                else:
                    wait_past(pe, h2_ready, 2 * i)
                for h in range(KD):
                    for t in range(NT):
                        ins = nc.tensor.transpose(tr[h][:, t * P:(t + 1) * P], z2[:, t, h * P:(h + 1) * P], ident[:])
                    ins.then_inc(z2_turned, 1)

            def ffn_in(b, j):
                i = CH * b + j
                pe.wait_ge(xk_ready, i + 1)
                wait_past(pe, th_ready, 2 * i)
                for dh in range(KD):
                    if dh == 1:
                        wait_past(pe, ro_ready, 2 * i - 1)
                    for ch in range(KD):
                        ins = mm(work[dh][:], w_ffn_t[:, 1, ch, dh * P:(dh + 1) * P], xk[:, ch], start=(ch == 0), stop=(ch == KD - 1))
                    ins.then_inc(k_done, 1)
                pe.wait_ge(xr_ready, i + 1)
                for q in range(2):
                    if q == 0:
                        wait_past(pe, ro_ready, 2 * i)
                    else:
                        pe.wait_ge(k_pos_ready, 2 * i + 1)
                    for t in (2 * q, 2 * q + 1):
                        for ch in range(KD):
                            ins = mm(work[2 - 2 * q][:, (t % 2) * D:(t % 2 + 1) * D], xr[:, ch, t * P:(t + 1) * P],
                                     w_ffn_t[:, 0, ch], start=(ch == 0), stop=(ch == KD - 1))
                    ins.then_inc(r_done, 1)

            def ffn_out(b, j):
                i = CH * b + j
                pe.wait_ge(now_ready, b + 1)
                pe.wait_ge(k_act_ready, i + 1)
                for q in range(2):
                    if q == 1:
                        pe.wait_ge(th_ready, 2 * i + 1)
                    for t in (2 * q, 2 * q + 1):
                        for ch in range(KD):
                            ins = mm(work[1 + q][:, (t % 2) * D:(t % 2 + 1) * D], k_act[:, ch, t * P:(t + 1) * P], wvf[:, ch],
                                     start=(ch == 0), stop=(ch == KD - 1))
                    ins.then_inc(o_done, 1)

            def turn_gram(b):
                pe.wait_ge(g_up_ready, b + 1)
                nc.tensor.transpose(gram[:, D + P:2 * D], g_sb[:, 0, P:D], ident[:]).then_inc(gram_turned, 1)

            def gram_q(b):
                pe.wait_ge(g_ready, b + 1)
                pe.wait_ge(qk_ready, b + 1)
                pe.wait_ge(edge_loaded, 32 * (b + 1))
                wait_past(pe, t_done, CH * b)
                for m in range(KD):
                    for k in range(KD):
                        ins = mm(att[m][:], g_sb[:, k, m * P:(m + 1) * P], wqk_aug[:, k, 0:HD], start=(k == 0), stop=(k == KD - 1))
                    ins.then_inc(gq_done, 1)

            def scores(b):
                pe.wait_ge(gq_ready, 2 * b + 2)
                for p in range(NP):
                    for m in range(KD):
                        ins = mm(gram[:, p * P:(p + 1) * P], gq[:, m, p * P:(p + 1) * P], wqk_aug[:, m, HD + p * P:HD + (p + 1) * P],
                                 start=(m == 0), stop=(m == KD - 1))
                ins.then_inc(score_done, 1)

            def wv_attn(b):
                pe.wait_ge(attn_ready, b + 1)
                pe.wait_ge(wv_ready, b + 1)
                for p in range(NP):
                    ins = mm(att[p // 2][:, (p % 2) * D:(p % 2 + 1) * D], attn[:, p], wv_aug[:, p], start=True, stop=True)
                    if p % 2:
                        ins.then_inc(pv_done, 1)

            def make_m(b):
                pe.wait_ge(pv_ready, 2 * b + 2)
                for k in range(KD):
                    for p in range(NP):
                        ins = mm(gram[:, k * D:(k + 1) * D], pv_t[:, p, k * P:(k + 1) * P], wfc_c[:, p], start=(p == 0), stop=(p == NP - 1))
                ins.then_inc(m_done, 1)

            def row_steps(b, last):
                n = b + 1
                for j in range(CH):
                    attention(b, j)
                    if j:
                        turn_z2(b, j - 1, last)
                    if not last:
                        gram_and_turn(n, j)
                    if j:
                        ffn_in(b, j - 1)
                    if not last and j == CH - 1:
                        turn_gram(n)
                    if j:
                        ffn_out(b, j - 1)
                turn_z2(b, CH - 1, last)
                if not last:
                    gram_q(n)
                    scores(n)
                ffn_in(b, CH - 1)
                if not last:
                    wv_attn(n)
                ffn_out(b, CH - 1)
                if not last:
                    make_m(n)

            setup()
            pe.wait_ge(w_copied, 5)
            for j in range(CH):
                gram_and_turn(0, j, first=True)
            turn_gram(0)
            gram_q(0)
            scores(0)
            wv_attn(0)
            pe.wait_ge(fc_ready, 1)
            make_m(0)
            row_steps(0, False)
            with pe.Fori(1, B - 1) as b:
                row_steps(b, False)
            row_steps(B - 1, True)


_INS = ['L0_attn_x', 'L0_attn_w_qkv', 'L0_attn_b_qkv', 'L0_attn_w_fc', 'L0_attn_b_fc', 'L0_attn_gamma', 'L0_attn_beta',
        'L0_ffn_W_r', 'L0_ffn_W_k', 'L0_ffn_W_v', 'L0_ffn_mu_r', 'L0_ffn_mu_k', 'L0_c', 'L0_wmod']


def kernel(**inputs):
    import numpy as _np
    import concourse.bacc as _bacc
    from concourse import mybir as _mybir
    from concourse.bass_utils import run_bass_kernel_spmd as _run

    nc = _bacc.Bacc("TRN2", target_bir_lowering=False, num_devices=1)
    arrays, args = {}, []
    for name in _INS:
        a = _np.ascontiguousarray(inputs[name])
        arrays[f"in_{name}_dram"] = a
        args.append(nc.dram_tensor(f"in_{name}_dram", a.shape, _mybir.dt.from_np(a.dtype), kind="ExternalInput").ap())
    shape = arrays["in_L0_attn_x_dram"].shape
    args.append(nc.dram_tensor("out_0_dram", shape, _mybir.dt.float32, kind="ExternalOutput").ap())
    adaln_block(nc, *args)
    r = _run(nc, [arrays], core_ids=[0])
    return r.results[0]["out_0_dram"]
```

```python
from contextlib import ExitStack

import concourse.bass as bass
from concourse import mybir

F32 = mybir.dt.float32
ALU = mybir.AluOpType
ACT = mybir.ActivationFunctionType
AX = mybir.AxisListType.X

P = 128


def adaln_block(nc, x, w_qkv, b_qkv, w_fc, b_fc, gamma, beta, w_r, w_k, w_v, mu_r, mu_k, c, wmod, out):
    B, L, D = x.shape
    HD = w_fc.shape[0]
    DX = 64
    H = HD // DX
    KD = D // P
    NP = H // 2
    CT = 512
    CH = L // CT
    NT = CT // P
    LAST = D - 1
    QK = 2 * HD
    SM_SCALE = float(DX) ** -0.5
    EPS_LN, EPS_ATT = 1e-5, 1e-6
    assert (KD, NP, NT, CH) == (2, 4, 4, 4)

    x_v = x.rearrange("b (j t p) d -> b j p t d", p=P, t=NT)
    out_v = out.rearrange("b (j t p) d -> b j p t d", p=P, t=NT)

    with ExitStack() as ctx:
        def sb(name, shape):
            return ctx.enter_context(nc.sbuf_tensor(name, shape, F32))

        def bank(name):
            return ctx.enter_context(nc.psum_tensor(name, [P, 512], F32))

        def sem(name):
            return ctx.enter_context(nc.semaphore(name))

        gram = bank("gram")
        tr = [bank(f"tr{h}") for h in range(KD)]
        att = [bank(f"att{q}") for q in range(2)]
        work = [bank(f"work{w}") for w in range(3)]

        ident = sb("ident", [P, P])
        ident_c = sb("ident_c", [P, KD, D])
        last_c = sb("last_c", [P, D])
        neg_half, half, quarter, minus_one, eps_att = (
            sb(n, [P, NT]) for n in ("neg_half", "half", "quarter", "minus_one", "eps_att"))
        wqkv_sb = sb("wqkv_sb", [P, KD, 3 * HD])
        wqk_last = sb("wqk_last", [P, QK])
        bv_col = sb("bv_col", [P, NP])
        wfc_c = sb("wfc_c", [P, NP, D])
        w_ffn_t = sb("w_ffn_t", [P, 3, KD, D])
        mu_col = sb("mu_col", [P, 2, KD])
        wv_t = sb("wv_t", [P, NP, D])

        th_c = sb("th_c", [P, KD * B])
        silu_u = sb("silu_u", [P, KD * B])
        silu = sb("silu", [P, KD * B])
        mod_col = sb("mod_col", [P, 8, B])
        vb_col = sb("vb_col", [P, NP, B])
        col8 = sb("col8", [B, 2])
        fc_mean = sb("fc_mean", [P, NP])
        scratch = nc.dram_tensor("row_scratch", [B, 4 * D + QK + D], F32)

        rows = sb("rows", [P, 4, D])
        g_row = sb("g_row", [P, D])
        mod_now = sb("mod_now", [P, 4])
        wvf = sb("wvf", [P, KD, D])
        d_now = sb("d_now", [P, KD])
        neg_d = sb("neg_d", [P, 1])
        wqk_l = sb("wqk_l", [P, QK])
        wqk_aug = sb("wqk_aug", [P, KD, QK])
        wv_mod = sb("wv_mod", [P, NP, D])
        wv_aug = sb("wv_aug", [P, NP, D])
        res_d = sb("res_d", [P, KD, D])
        res = sb("res", [P, KD, D])
        g_sb = sb("g_sb", [P, KD, D])
        gq = sb("gq", [P, KD, HD])
        s_max = sb("s_max", [P, NP])
        s_dif = sb("s_dif", [P, NP, DX])
        s_exp = sb("s_exp", [P, NP, DX])
        s_sum = sb("s_sum", [P, NP])
        s_inv = sb("s_inv", [P, NP])
        attn = sb("attn", [P, NP, P])
        pv_t = sb("pv_t", [P, NP, D])
        m_sb = sb("m_sb", [P, KD, D])

        x_in = sb("x_in", [P, CH, NT, D])
        xb = sb("xb", [P, CH, NT, D])
        z = sb("z", [P, 2, NT, D])
        z_t = sb("z_t", [P, CH, KD, CT])
        st_a = sb("st_a", [P, CH, NT, 6])
        ag_a = sb("ag_a", [P, CH, 8, NT])
        sq_junk = ctx.enter_context(nc.sbuf_tensor("sq_junk", [P, NT, D], mybir.dt.bfloat16))
        ssq = sb("ssq", [P, 2, NT])
        ve_o = sb("ve_o", [P, 2, NT])
        rs_o = sb("rs_o", [P, 2, NT])
        t_buf = sb("t_buf", [P, NT, D])
        x2 = sb("x2", [P, CH, NT, D])
        st_2 = sb("st_2", [P, 2, NT, 6])
        ag_2 = sb("ag_2", [P, 2, 8, NT])
        z2 = sb("z2", [P, NT, D])
        h2t = sb("h2t", [P, KD, 1 + L])
        xk = sb("xk", [P, KD, CT])
        xr = sb("xr", [P, KD, CT])
        k_act = sb("k_act", [P, KD, CT])
        th_r = sb("th_r", [P, NT, D])
        y = sb("y", [P, 2, NT, D])

        dif = t_buf[:].rearrange("p t d -> p (t d)").rearrange("p (k n) -> p k n", k=KD)

        wmod_sb = x2[:, 0:3].rearrange("p j t d -> p (j t d)").rearrange("p (k n) -> p k n", k=KD)
        w_ffn = y[:].rearrange("p s t d -> p (s t d)")[:, 0:3 * KD * D].rearrange(
            "p (n k d) -> p n k d", n=3, k=KD)
        NR = 5 * D + QK
        room8 = xb[0:B].rearrange("p j t d -> p (j t d)")
        row8 = room8[:, 0:NR]
        tmp8 = room8[:, NR:NR + 4 * D].rearrange("p (n d) -> p n d", n=4)
        bqk8 = z2[0:B].rearrange("p t d -> p (t d)")
        c_sb, gamma8, beta8, bfc8 = (t_buf[0:B, n] for n in range(4))

        ident_ready = sem("ident_ready")
        const_ready = sem("const_ready")
        pool_step = sem("pool_step")
        c_loaded = sem("c_loaded")
        wmod_loaded = sem("wmod_loaded")
        wqkv_loaded = sem("wqkv_loaded")
        small_loaded = sem("small_loaded")
        wfc_loaded = sem("wfc_loaded")
        ffn_loaded = sem("ffn_loaded")
        c_turned = sem("c_turned")
        c_tanh = sem("c_tanh")
        silu_ready = sem("silu_ready")
        mod_done = sem("mod_done")
        mod_col_ready = sem("mod_col_ready")
        bias_done = sem("bias_done")
        row8_step = sem("row8_step")
        row8_ready = sem("row8_ready")
        vb_ready = sem("vb_ready")
        fc_step = sem("fc_step")
        fc_ready = sem("fc_ready")
        w_turned = sem("w_turned")
        w_copied = sem("w_copied")
        row8_stored = sem("row8_stored")
        rows_loaded = sem("rows_loaded")
        edge_loaded = sem("edge_loaded")
        now_ready = sem("now_ready")
        prep_step = sem("prep_step")
        qk_ready = sem("qk_ready")
        wv_step = sem("wv_step")
        wv_ready = sem("wv_ready")
        g_up_ready = sem("g_up_ready")
        gram_turned = sem("gram_turned")
        g_ready = sem("g_ready")
        gq_done = sem("gq_done")
        gq_ready = sem("gq_ready")
        score_done = sem("score_done")
        sm_step = sem("sm_step")
        s_dif_ready = sem("s_dif_ready")
        exp_done = sem("exp_done")
        attn_ready = sem("attn_ready")
        pv_done = sem("pv_done")
        pv_ready = sem("pv_ready")
        m_done = sem("m_done")
        m_ready = sem("m_ready")
        x_loaded = [sem(f"x_loaded{j}") for j in range(CH)]
        st_a_done = sem("st_a_done")
        ag_a_step = sem("ag_a_step")
        rs_a_ready = sem("rs_a_ready")
        z_ready = sem("z_ready")
        z_turned = sem("z_turned")
        z_used = sem("z_used")
        z_t_ready = sem("z_t_ready")
        xb_ready = sem("xb_ready")
        att_done = sem("att_done")
        ssq_ready = sem("ssq_ready")
        ve_o_done = sem("ve_o_done")
        rs_o_ready = sem("rs_o_ready")
        t_done = sem("t_done")
        x2_ready = sem("x2_ready")
        st_2_done = sem("st_2_done")
        ag_2_step = sem("ag_2_step")
        rs_2_step = sem("rs_2_step")
        rs_2_ready = sem("rs_2_ready")
        z2_ready = sem("z2_ready")
        z2_turned = sem("z2_turned")
        h2_ready = sem("h2_ready")
        dif_done = sem("dif_done")
        xk_ready = sem("xk_ready")
        xr_ready = sem("xr_ready")
        k_done = sem("k_done")
        k_pos_ready = sem("k_pos_ready")
        k_act_ready = sem("k_act_ready")
        r_done = sem("r_done")
        th_ready = sem("th_ready")
        o_done = sem("o_done")
        ro_ready = sem("ro_ready")
        y_ready = sem("y_ready")
        y_stored = [sem(f"y_stored{s}") for s in range(2)]

        def wait_past(eng, semaphore, count):
            if not isinstance(count, int) or count > 0:
                eng.wait_ge(semaphore, count)

        block = ctx.enter_context(nc.Block())

        @block.sync
        def _(sp):
            def load_x(b, j):
                sp.dma_start(x_in[:, j], x_v[b, j]).then_inc(x_loaded[j], 16)

            def load_rows(b):
                src = scratch[b, 0:4 * D].partition_broadcast(P)
                sp.dma_start(rows[:].rearrange("p r d -> p (r d)"), src).then_inc(rows_loaded, 16)
                sp.dma_start(wqk_aug[P - 1:P, KD - 1, :], scratch[b, 4 * D:4 * D + QK].unsqueeze(0)).then_inc(edge_loaded, 16)
                sp.dma_start(res[P - 1:P, KD - 1, :], scratch[b, 4 * D + QK:5 * D + QK].unsqueeze(0)).then_inc(edge_loaded, 16)

            def next_x(b, j):
                sp.wait_ge(z_ready, CH * (b - 1) + j + 1)
                sp.wait_ge(xb_ready, CH * (b - 1) + j + 1)
                load_x(b, j)

            def next_rows(b):
                sp.wait_ge(xb_ready, CH * b)
                sp.wait_ge(now_ready, b)
                sp.wait_ge(m_ready, b)
                load_rows(b)

            def store_y(b, j):
                sp.wait_ge(y_ready, CH * b + j + 1)
                sp.dma_start(out_v[b, j], y[:, j % 2]).then_inc(y_stored[j % 2], 16)

            def row_steps(b):
                next_rows(b + 1)
                next_x(b + 2, 0)
                next_x(b + 2, 1)
                next_x(b + 2, 2)
                store_y(b, 0)
                next_x(b + 2, 3)
                for j in range(1, CH):
                    store_y(b, j)

            sp.dma_start(c_sb, c).then_inc(c_loaded, 16)
            sp.dma_start(wmod_sb, wmod.rearrange("(k p) n -> p k n", p=P)).then_inc(wmod_loaded, 16)
            for j in range(CH):
                load_x(0, j)
            sp.dma_start(w_ffn[:, 0], w_r.rearrange("(k p) n -> p k n", p=P)).then_inc(ffn_loaded, 16)
            sp.dma_start(w_ffn[:, 1], w_k.rearrange("(k p) n -> p k n", p=P)).then_inc(ffn_loaded, 16)
            sp.dma_start(w_ffn[:, 2], w_v.rearrange("(k p) n -> p k n", p=P)).then_inc(ffn_loaded, 16)
            sp.wait_ge(row8_ready, 1)
            sp.dma_start(scratch[:, :], row8).then_inc(row8_stored, 16)
            sp.wait_ge(row8_stored, 16)
            load_rows(0)
            for j in range(CH):
                next_x(1, j)
            row_steps(0)
            with sp.Fori(1, B - 2) as b:
                row_steps(b)
            next_rows(B - 1)
            for b in (B - 2, B - 1):
                for j in range(CH):
                    store_y(b, j)
            for s in range(2):
                sp.wait_ge(y_stored[s], 16 * B * CH // 2)

        @block.gpsimd
        def _(pool):
            def build_constants():
                nc.gpsimd.memset(ident[:], 0.0).then_inc(pool_step, 1)
                nc.gpsimd.memset(ident_c[:], -1.0 / D).then_inc(pool_step, 1)
                nc.gpsimd.memset(last_c[:], -1.0 / D).then_inc(pool_step, 1)
                pool.wait_ge(pool_step, 3)
                nc.gpsimd.affine_select(out=ident[:], in_=ident[:], compare_op=ALU.not_equal, fill=1.0, base=0,
                                        pattern=[[-1, P]], channel_multiplier=1).then_inc(ident_ready, 1)
                nc.gpsimd.affine_select(out=ident_c[:], in_=ident_c[:], compare_op=ALU.not_equal, fill=1.0 - 1.0 / D,
                                        base=0, pattern=[[P, KD], [-1, D]], channel_multiplier=1).then_inc(const_ready, 1)
                nc.gpsimd.memset(last_c[:, LAST:D], 1.0 - 1.0 / D).then_inc(const_ready, 1)
                nc.gpsimd.memset(half[:], 0.5).then_inc(const_ready, 1)
                nc.gpsimd.memset(minus_one[:], -1.0).then_inc(const_ready, 1)
                nc.gpsimd.memset(quarter[:], 0.25).then_inc(const_ready, 1)
                nc.gpsimd.memset(eps_att[:], EPS_ATT).then_inc(const_ready, 1)
                nc.gpsimd.memset(neg_half[:], -0.5).then_inc(const_ready, 1)
                nc.gpsimd.memset(attn[:], 0.0).then_inc(const_ready, 1)
                nc.gpsimd.memset(h2t[:, :, 0:1], 0.0).then_inc(const_ready, 1)
                nc.gpsimd.memset(z[:, :, :, LAST:D], 1.0).then_inc(const_ready, 1)
                pool.wait_ge(const_ready, 10)

            def layernorm_factors(i, st, ag, st_done, ag_step, ready, eps):
                pool.wait_ge(st_done, i + 1)
                nc.gpsimd.tensor_tensor(ag[:, 0], st[:, :, 1], st[:, :, 4], ALU.add)
                nc.gpsimd.tensor_tensor(ag[:, 1], st[:, :, 1], st[:, :, 4], ALU.subtract)
                nc.gpsimd.tensor_tensor(ag[:, 2], st[:, :, 2], st[:, :, 5], ALU.add).then_inc(ag_step, 1)
                pool.wait_ge(ag_step, 4 * i + 1)
                nc.gpsimd.tensor_tensor(ag[:, 3], ag[:, 0], half[:], ALU.mult)
                nc.gpsimd.tensor_tensor(ag[:, 4], ag[:, 1], ag[:, 1], ALU.mult)
                nc.gpsimd.tensor_scalar(ag[:, 5], ag[:, 2], 1.0 / D, eps, ALU.mult, ALU.add).then_inc(ag_step, 1)
                pool.wait_ge(ag_step, 4 * i + 2)
                nc.gpsimd.tensor_tensor(ag[:, 4], ag[:, 4], quarter[:], ALU.mult).then_inc(ag_step, 1)
                pool.wait_ge(ag_step, 4 * i + 3)
                nc.gpsimd.tensor_tensor(ag[:, 6], ag[:, 4], ag[:, 5], ALU.add).then_inc(ag_step, 1)
                pool.wait_ge(ag_step, 4 * i + 4)
                nc.gpsimd.tensor_tensor(ag[:, 7], ag[:, 6], neg_half[:], ALU.pow).then_inc(ready, 1)

            def rstd_a(b, j):
                layernorm_factors(CH * b + j, st_a[:, j], ag_a[:, j], st_a_done, ag_a_step, rs_a_ready, EPS_LN)

            def rstd_2(b, j):
                i, ag = CH * b + j, ag_2[:, j % 2]
                layernorm_factors(i, st_2[:, j % 2], ag, st_2_done, ag_2_step, rs_2_step, EPS_LN)
                nc.gpsimd.tensor_tensor(ag[:, 0], ag[:, 3], minus_one[:], ALU.mult).then_inc(rs_2_step, 1)
                pool.wait_ge(rs_2_step, 2 * i + 2)
                nc.gpsimd.tensor_tensor(ag[:, 1], ag[:, 0], ag[:, 7], ALU.mult).then_inc(rs_2_ready, 1)

            def rstd_o(b, j):
                i, s = CH * b + j, j % 2
                pool.wait_ge(ssq_ready, i + 1)
                nc.gpsimd.tensor_tensor(ve_o[:, s], ssq[:, s], eps_att[:], ALU.add).then_inc(ve_o_done, 1)
                pool.wait_ge(ve_o_done, i + 1)
                nc.gpsimd.tensor_tensor(rs_o[:, s], ve_o[:, s], neg_half[:], ALU.pow).then_inc(rs_o_ready, 1)

            def make_xb(b, j, first=False):
                pool.wait_ge(x_loaded[j], 16 * (b + 1))
                pool.wait_ge(rows_loaded, 16 * (b + 1))
                if not first:
                    pool.wait_ge(x2_ready, CH * (b - 1) + j + 1)
                nc.gpsimd.tensor_tensor(xb[:, j], x_in[:, j], rows[:, 2].unsqueeze(1).to_broadcast([P, NT, D]),
                                        ALU.add).then_inc(xb_ready, 1)

            def prep_wv(b):
                pool.wait_ge(rows_loaded, 16 * (b + 1))
                wait_past(pool, m_ready, b)
                nc.gpsimd.tensor_tensor(wv_mod[:], wv_t[:], rows[:, 0].unsqueeze(1).to_broadcast([P, NP, D]),
                                        ALU.mult).then_inc(wv_step, 1)
                pool.wait_ge(wv_step, b + 1)
                nc.gpsimd.tensor_tensor(wv_aug[:, :, 0:LAST], wv_mod[:, :, 0:LAST],
                                        wv_mod[:, :, LAST:D].to_broadcast([P, NP, LAST]), ALU.subtract)
                nc.gpsimd.tensor_copy(wv_aug[:, :, LAST], vb_col[:, :, b]).then_inc(wv_ready, 1)

            def add_y(b, j):
                i, s = CH * b + j, j % 2
                pool.wait_ge(ro_ready, 2 * i + 2)
                nc.gpsimd.tensor_tensor(y[:, s], y[:, s], x2[:, j], ALU.add).then_inc(y_ready, 1)

            def row_steps(b, near, far):
                n = b + 1
                rstd_o(b, 0)
                rstd_2(b, 0)
                rstd_o(b, 1)
                if near:
                    make_xb(n, 0)
                rstd_2(b, 1)
                rstd_o(b, 2)
                if near:
                    make_xb(n, 1)
                rstd_2(b, 2)
                if near:
                    make_xb(n, 2)
                add_y(b, 0)
                rstd_o(b, 3)
                rstd_2(b, 3)
                if near:
                    make_xb(n, 3)
                if far:
                    rstd_a(n + 1, 0)
                    rstd_a(n + 1, 1)
                if near:
                    prep_wv(n)
                add_y(b, 1)
                if far:
                    rstd_a(n + 1, 2)
                    rstd_a(n + 1, 3)
                add_y(b, 2)
                add_y(b, 3)

            build_constants()
            for j in range(CH):
                rstd_a(0, j)
            pool.wait_ge(w_copied, 5)
            pool.wait_ge(vb_ready, 1)
            prep_wv(0)
            for j in range(CH):
                make_xb(0, j, first=True)
            for j in range(CH):
                rstd_a(1, j)
            row_steps(0, True, True)
            with pool.Fori(1, B - 2) as b:
                row_steps(b, True, True)
            row_steps(B - 2, True, False)
            row_steps(B - 1, False, False)

        @block.scalar
        def _(act):
            def load_weights():
                act.dma_start(wqkv_sb[:], w_qkv.rearrange("(k p) n -> p k n", p=P)).then_inc(wqkv_loaded, 16)
                act.dma_start(bqk8, b_qkv[0:QK].partition_broadcast(B)).then_inc(small_loaded, 16)
                act.dma_start(gamma8, gamma.partition_broadcast(B)).then_inc(small_loaded, 16)
                act.dma_start(beta8, beta.partition_broadcast(B)).then_inc(small_loaded, 16)
                act.dma_start(bfc8, b_fc.partition_broadcast(B)).then_inc(small_loaded, 16)
                act.dma_start(wqk_last[:], w_qkv[LAST, 0:QK].partition_broadcast(P)).then_inc(small_loaded, 16)
                with nc.allow_non_contiguous_dma(reason="three short vectors onto partitions"):
                    act.dma_start(bv_col[:], b_qkv[QK:3 * HD].rearrange("(n p) -> p n", p=P)).then_inc(small_loaded, 16)
                    act.dma_start(mu_col[:, 0], mu_r.rearrange("(k p) -> p k", p=P)).then_inc(small_loaded, 16)
                    act.dma_start(mu_col[:, 1], mu_k.rearrange("(k p) -> p k", p=P)).then_inc(small_loaded, 16)
                act.dma_start(wfc_c[:], w_fc.rearrange("(n p) d -> p n d", p=P)).then_inc(wfc_loaded, 16)

            def setup():
                act.wait_ge(c_turned, 1)
                nc.scalar.activation(th_c[:], work[0][:, 0:KD * B], ACT.Tanh, scale=0.5).then_inc(c_tanh, 1)
                for n, (dst, src) in enumerate([
                        (wv_t[:, 0:2], gram), (wv_t[:, 2:4], att[0]),
                        (w_ffn_t[:, 0], work[0]), (w_ffn_t[:, 1], work[1]), (w_ffn_t[:, 2], work[2])]):
                    act.wait_ge(w_turned, n + 1)
                    nc.scalar.activation(dst.rearrange("p a d -> p (a d)"), src[:], ACT.Copy).then_inc(w_copied, 1)

            def copy_z_t(b, j):
                i = CH * b + j
                for h in range(KD):
                    act.wait_ge(z_turned, 2 * i + h + 1)
                    nc.scalar.activation(z_t[:, j, h], tr[h][:], ACT.Copy).then_inc(z_t_ready, 1)

            def copy_gram(b):
                act.wait_ge(z_used, CH * (b + 1))
                nc.scalar.activation(g_sb[:, 0], gram[:, 0:D], ACT.Copy)
                nc.scalar.activation(g_sb[:, 1, P:D], gram[:, D:D + P], ACT.Copy).then_inc(g_up_ready, 1)

            def copy_gram_low(b):
                act.wait_ge(gram_turned, b + 1)
                nc.scalar.activation(g_sb[:, 1, 0:P], gram[:, D + P:2 * D], ACT.Copy).then_inc(g_ready, 1)

            def copy_gq(b):
                for m in range(KD):
                    act.wait_ge(gq_done, 2 * b + m + 1)
                    nc.scalar.activation(gq[:, m], att[m][:], ACT.Copy).then_inc(gq_ready, 1)

            def exps(b):
                act.wait_ge(s_dif_ready, b + 1)
                nc.scalar.activation(s_exp[:], s_dif[:], ACT.Exp, scale=SM_SCALE).then_inc(exp_done, 1)

            def copy_pv(b):
                for g in range(2):
                    act.wait_ge(pv_done, 2 * b + g + 1)
                    nc.scalar.activation(pv_t[:, 2 * g:2 * g + 2].rearrange("p n d -> p (n d)"), att[g][:],
                                         ACT.Copy).then_inc(pv_ready, 1)

            def squares(b, j):
                i, s = CH * b + j, j % 2
                for t in range(NT):
                    if t % 2 == 0:
                        act.wait_ge(att_done, 2 * i + t // 2 + 1)
                    sq = nc.scalar.activation(sq_junk[:, t], att[t // 2][:, (t % 2) * D:(t % 2 + 1) * D], ACT.Square,
                                              scale=float(D) ** -0.5, accum_out=ssq[:, s, t:t + 1])
                sq.then_inc(ssq_ready, 1)

            def copy_h2(b, j):
                i = CH * b + j
                for h in range(KD):
                    act.wait_ge(z2_turned, 2 * i + h + 1)
                    nc.scalar.activation(h2t[:, h, 1 + j * CT:1 + (j + 1) * CT], tr[h][:], ACT.Identity,
                                         bias=mod_now[:, h:h + 1], scale=mod_now[:, 2 + h:3 + h]).then_inc(h2_ready, 1)

            def k_and_r(b, j):
                i = CH * b + j
                for h in range(KD):
                    act.wait_ge(k_done, 2 * i + h + 1)
                    nc.scalar.activation(k_act[:, h], work[h][:], ACT.Relu).then_inc(k_pos_ready, 1)
                act.wait_ge(k_pos_ready, 2 * i + 2)
                nc.scalar.activation(k_act[:], k_act[:], ACT.Square).then_inc(k_act_ready, 1)
                for q in range(2):
                    act.wait_ge(r_done, 2 * i + q + 1)
                    nc.scalar.activation(th_r[:, 2 * q:2 * q + 2].rearrange("p t d -> p (t d)"), work[2 - 2 * q][:],
                                         ACT.Tanh, scale=0.5).then_inc(th_ready, 1)

            def make_z2(b, j):
                i, s = CH * b + j, j % 2
                act.wait_ge(rs_2_ready, i + 1)
                for t in range(NT):
                    ins = nc.scalar.activation(z2[:, t], x2[:, j, t], ACT.Identity, bias=ag_2[:, s, 1, t:t + 1],
                                               scale=ag_2[:, s, 7, t:t + 1])
                ins.then_inc(z2_ready, 1)

            def row_steps(b, near):
                n = b + 1
                for j in range(CH):
                    squares(b, j)
                    if near:
                        copy_z_t(n, j)
                    if j:
                        make_z2(b, j - 1)
                    if near and j == CH - 1:
                        copy_gram(n)
                    if j > 1:
                        k_and_r(b, j - 2)
                    if near and j == CH - 1:
                        copy_gram_low(n)
                    if j:
                        copy_h2(b, j - 1)
                make_z2(b, CH - 1)
                if near:
                    copy_gq(n)
                k_and_r(b, CH - 2)
                copy_h2(b, CH - 1)
                if near:
                    exps(n)
                    copy_pv(n)
                k_and_r(b, CH - 1)

            load_weights()
            setup()
            for j in range(CH):
                copy_z_t(0, j)
            copy_gram(0)
            copy_gram_low(0)
            copy_gq(0)
            exps(0)
            copy_pv(0)
            row_steps(0, True)
            with act.Fori(1, B - 1) as b:
                row_steps(b, True)
            row_steps(B - 1, False)

        @block.vector
        def _(dve):
            def setup():
                dve.wait_ge(c_tanh, 1)
                nc.vector.scalar_tensor_tensor(silu_u[:], th_c[:], 1.0, work[0][:, 0:KD * B], ALU.add,
                                               ALU.mult).then_inc(row8_step, 1)
                dve.wait_ge(row8_step, 1)
                nc.vector.tensor_scalar(silu[:], silu_u[:], 0.5, None, ALU.mult).then_inc(silu_ready, 1)
                dve.wait_ge(mod_done, 1)
                flat = mod_col[:].rearrange("p m b -> p (m b)")
                w = KD * B
                for m, add in enumerate((0.0, 1.0, 0.0, 1.0)):
                    ins = nc.vector.tensor_scalar(flat[:, m * w:(m + 1) * w], att[0][:, m * w:(m + 1) * w], add, None, ALU.add)
                ins.then_inc(mod_col_ready, 1)
                dve.wait_ge(small_loaded, 16 * 8)
                nc.vector.tensor_scalar(row8[:, 0:D], work[0][0:B, D:2 * D], 1.0, None, ALU.add)
                steps = 1
                for n, src in enumerate((work[1][0:B, 0:D], work[2][0:B, D:2 * D])):
                    size, sign = tmp8[:, 2 * n], tmp8[:, 2 * n + 1]
                    nc.vector.tensor_scalar(sign, src, -1.0, None, ALU.mult).then_inc(row8_step, 1)
                    dve.wait_ge(row8_step, steps + 1)
                    nc.vector.tensor_tensor(size, sign, src, ALU.max).then_inc(row8_step, 1)
                    dve.wait_ge(row8_step, steps + 2)
                    nc.vector.tensor_scalar(sign, src, 0.0, 2.0, ALU.is_ge, ALU.mult).then_inc(row8_step, 1)
                    nc.vector.tensor_scalar(size, size, 0.25, None, ALU.max).then_inc(row8_step, 1)
                    dve.wait_ge(row8_step, steps + 4)
                    nc.vector.scalar_tensor_tensor(size, sign, -1.0, size, ALU.add, ALU.mult).then_inc(row8_step, 1)
                    dve.wait_ge(row8_step, steps + 5)
                    steps += 5
                nc.vector.tensor_tensor(row8[:, D:2 * D], tmp8[:, 0], gamma8, ALU.mult)
                nc.vector.tensor_tensor(row8[:, 2 * D:3 * D], tmp8[:, 0], beta8, ALU.mult)
                nc.vector.tensor_scalar(row8[:, 3 * D:4 * D], tmp8[:, 2], 0.5, None, ALU.mult)
                e = 4 * D + QK
                nc.vector.scalar_tensor_tensor(row8[:, e:e + D], work[0][0:B, 0:D], 0.0, bfc8, ALU.add, ALU.add,
                                               accum_out=col8[:, 0:1]).then_inc(row8_step, 1)
                dve.wait_ge(row8_step, steps + 1)
                nc.vector.tensor_scalar(col8[:, 1:2], col8[:, 0:1], 1.0 / D, None, ALU.mult).then_inc(row8_step, 1)
                dve.wait_ge(row8_step, steps + 2)
                nc.vector.tensor_scalar(row8[:, e:e + D], row8[:, e:e + D], col8[:, 1:2], None,
                                        ALU.subtract).then_inc(row8_step, 1)
                dve.wait_ge(bias_done, 1)
                for g in range(2):
                    ins = nc.vector.tensor_tensor(row8[:, 4 * D + g * HD:4 * D + (g + 1) * HD], tr[g][0:B, :],
                                                  bqk8[:, g * HD:(g + 1) * HD], ALU.add)
                ins.then_inc(row8_ready, 1)
                for p in range(NP):
                    ins = nc.vector.tensor_scalar(vb_col[:, p], att[1][:, p * B:(p + 1) * B], bv_col[:, p:p + 1], None, ALU.add)
                ins.then_inc(vb_ready, 1)
                dve.wait_ge(wfc_loaded, 16)
                nc.vector.tensor_reduce(fc_mean[:], wfc_c[:], AX, ALU.add).then_inc(fc_step, 1)
                dve.wait_ge(fc_step, 1)
                nc.vector.tensor_scalar(fc_mean[:], fc_mean[:], 1.0 / D, None, ALU.mult).then_inc(fc_step, 1)
                dve.wait_ge(fc_step, 2)
                for p in range(NP):
                    ins = nc.vector.tensor_scalar(wfc_c[:, p], wfc_c[:, p], fc_mean[:, p:p + 1], None, ALU.subtract)
                ins.then_inc(fc_ready, 1)

            def stats_a(b, j):
                i = CH * b + j
                dve.wait_ge(x_loaded[j], 16 * (b + 1))
                for t in range(NT):
                    ins = nc.vector.bn_stats(st_a[:, j, t], x_in[:, j, t])
                ins.then_inc(st_a_done, 1)

            def make_z(b, j, first=False):
                i = CH * b + j
                dve.wait_ge(rs_a_ready, i + 1)
                if not (first and j < 2):
                    dve.wait_ge(z_used, i - 1)
                for t in range(NT):
                    ins = nc.vector.tensor_scalar(z[:, j % 2, t, 0:LAST], x_in[:, j, t, 0:LAST], ag_a[:, j, 3, t:t + 1],
                                                  ag_a[:, j, 7, t:t + 1], ALU.subtract, ALU.mult)
                ins.then_inc(z_ready, 1)

            def make_x2(b, j):
                i, s = CH * b + j, j % 2
                wait_past(dve, xr_ready, CH * b + max(j - 1, 0))
                dve.wait_ge(rs_o_ready, i + 1)
                for t in range(NT):
                    ins = nc.vector.scalar_tensor_tensor(t_buf[:, t], att[t // 2][:, (t % 2) * D:(t % 2 + 1) * D],
                                                         rs_o[:, s, t:t + 1], g_row[:], ALU.mult, ALU.mult)
                ins.then_inc(t_done, 1)
                dve.wait_ge(t_done, i + 1)
                dve.wait_ge(xb_ready, i + 1)
                nc.vector.tensor_tensor(x2[:, j], t_buf[:], xb[:, j], ALU.add).then_inc(x2_ready, 1)

            def stats_2(b, j):
                i, s = CH * b + j, j % 2
                dve.wait_ge(x2_ready, i + 1)
                for t in range(NT):
                    ins = nc.vector.bn_stats(st_2[:, s, t], x2[:, j, t])
                ins.then_inc(st_2_done, 1)

            def mix(b, j):
                i = CH * b + j
                dve.wait_ge(h2_ready, 2 * i + 2)
                prev = h2t[:, :, j * CT:(j + 1) * CT]
                nc.vector.tensor_tensor(dif, h2t[:, :, 1 + j * CT:1 + (j + 1) * CT], prev, ALU.subtract).then_inc(dif_done, 1)
                dve.wait_ge(dif_done, i + 1)
                for n, (dst, ready) in enumerate(((xk, xk_ready), (xr, xr_ready))):
                    for h in range(KD):
                        ins = nc.vector.scalar_tensor_tensor(dst[:, h], dif[:, h], mu_col[:, 1 - n, h:h + 1], prev[:, h],
                                                             ALU.mult, ALU.add)
                    ins.then_inc(ready, 1)

            def gate_o(b, j):
                i, s = CH * b + j, j % 2
                wait_past(dve, y_stored[s], 16 * (2 * b + j // 2))
                dve.wait_ge(th_ready, 2 * i + 2)
                for q in range(2):
                    dve.wait_ge(o_done, 2 * i + q + 1)
                    nc.vector.scalar_tensor_tensor(y[:, s, 2 * q:2 * q + 2].rearrange("p t d -> p (t d)"),
                                                   th_r[:, 2 * q:2 * q + 2].rearrange("p t d -> p (t d)"), 1.0,
                                                   work[1 + q][:], ALU.add, ALU.mult).then_inc(ro_ready, 1)

            def take_rows(b):
                nc.vector.tensor_copy(g_row[:], rows[:, 1])
                nc.vector.tensor_copy(mod_now[:], mod_col[:, 4:8, b])
                nc.vector.tensor_tensor(wvf[:], w_ffn_t[:, 2], rows[:, 3].unsqueeze(1).to_broadcast([P, KD, D]),
                                        ALU.mult).then_inc(now_ready, 1)
                dve.wait_ge(now_ready, b + 1)

            def prep_qk(b):
                dve.wait_ge(rows_loaded, 16 * (b + 1))
                nc.vector.tensor_scalar(neg_d[:], rows[:, 0, LAST:D], -1.0, None, ALU.mult).then_inc(prep_step, 1)
                nc.vector.tensor_copy(d_now[:], mod_col[:, 2:4, b]).then_inc(prep_step, 1)
                dve.wait_ge(prep_step, 4 * b + 2)
                nc.vector.tensor_scalar(wqk_l[:], wqk_last[:], neg_d[:], None, ALU.mult).then_inc(prep_step, 1)
                for k in range(KD):
                    ins = nc.vector.tensor_scalar(res_d[:, k], ident_c[:, k], d_now[:, k:k + 1], None, ALU.mult)
                ins.then_inc(prep_step, 1)
                dve.wait_ge(prep_step, 4 * b + 4)
                for k in range(KD):
                    n = P if k < KD - 1 else P - 1
                    nc.vector.scalar_tensor_tensor(wqk_aug[0:n, k], wqkv_sb[0:n, k, 0:QK], d_now[0:n, k:k + 1],
                                                   wqk_l[0:n], ALU.mult, ALU.add)
                    ins = nc.vector.scalar_tensor_tensor(res[0:n, k], last_c[0:n], neg_d[0:n], res_d[0:n, k],
                                                         ALU.mult, ALU.add)
                ins.then_inc(qk_ready, 1)

            def softmax_dif(b):
                dve.wait_ge(score_done, b + 1)
                for g in range(2):
                    lo = g * DX
                    block = gram[lo:lo + DX, :].rearrange("p (n e) -> p n e", n=NP)[:, :, lo:lo + DX]
                    nc.vector.tensor_reduce(s_max[lo:lo + DX], block, AX, ALU.max).then_inc(sm_step, 1)
                dve.wait_ge(sm_step, 4 * b + 2)
                for g in range(2):
                    lo = g * DX
                    block = gram[lo:lo + DX, :].rearrange("p (n e) -> p n e", n=NP)[:, :, lo:lo + DX]
                    ins = nc.vector.tensor_tensor(s_dif[lo:lo + DX], block,
                                                  s_max[lo:lo + DX].unsqueeze(2).to_broadcast([DX, NP, DX]), ALU.subtract)
                ins.then_inc(s_dif_ready, 1)

            def softmax_norm(b):
                dve.wait_ge(exp_done, b + 1)
                nc.vector.tensor_reduce(s_sum[:], s_exp[:], AX, ALU.add).then_inc(sm_step, 1)
                dve.wait_ge(sm_step, 4 * b + 3)
                nc.vector.reciprocal(s_inv[:], s_sum[:]).then_inc(sm_step, 1)
                dve.wait_ge(sm_step, 4 * b + 4)
                for g in range(2):
                    lo = g * DX
                    ins = nc.vector.tensor_tensor(attn[lo:lo + DX, :, lo:lo + DX], s_exp[lo:lo + DX],
                                                  s_inv[lo:lo + DX].unsqueeze(2).to_broadcast([DX, NP, DX]), ALU.mult)
                ins.then_inc(attn_ready, 1)

            def make_m(b):
                dve.wait_ge(m_done, b + 1)
                dve.wait_ge(edge_loaded, 32 * (b + 1))
                nc.vector.tensor_tensor(m_sb[:].rearrange("p k d -> p (k d)"), gram[:],
                                        res[:].rearrange("p k d -> p (k d)"), ALU.add).then_inc(m_ready, 1)

            def row_steps(b, near, far):
                n = b + 1
                take_rows(b)
                make_x2(b, 0)
                stats_2(b, 0)
                if near:
                    make_z(n, 2)
                make_x2(b, 1)
                stats_2(b, 1)
                mix(b, 0)
                if near:
                    make_z(n, 3)
                make_x2(b, 2)
                stats_2(b, 2)
                if near:
                    prep_qk(n)
                mix(b, 1)
                gate_o(b, 0)
                make_x2(b, 3)
                stats_2(b, 3)
                if far:
                    for j in range(2):
                        stats_a(n + 1, j)
                    for j in range(2):
                        make_z(n + 1, j)
                mix(b, 2)
                gate_o(b, 1)
                if far:
                    for j in range(2, CH):
                        stats_a(n + 1, j)
                if near:
                    softmax_dif(n)
                    softmax_norm(n)
                mix(b, 3)
                gate_o(b, 2)
                if near:
                    make_m(n)
                gate_o(b, 3)

            setup()
            dve.wait_ge(const_ready, 10)
            dve.wait_ge(wqkv_loaded, 16)
            dve.wait_ge(w_copied, 5)
            stats_a(0, 0)
            stats_a(0, 1)
            make_z(0, 0, first=True)
            stats_a(0, 2)
            make_z(0, 1, first=True)
            stats_a(0, 3)
            prep_qk(0)
            make_z(0, 2, first=True)
            make_z(0, 3, first=True)
            softmax_dif(0)
            softmax_norm(0)
            make_m(0)
            for j in range(CH):
                stats_a(1, j)
            make_z(1, 0)
            make_z(1, 1)
            row_steps(0, True, True)
            with dve.Fori(1, B - 2) as b:
                row_steps(b, True, True)
            row_steps(B - 2, True, False)
            row_steps(B - 1, False, False)

        @block.tensor
        def _(pe):
            mm = nc.tensor.matmul

            def setup():
                pe.wait_ge(ident_ready, 1)
                pe.wait_ge(c_loaded, 16)
                for k in range(KD):
                    ins = nc.tensor.transpose(work[0][:, k * B:(k + 1) * B], c_sb[:, k * P:(k + 1) * P], ident[0:B, 0:B])
                ins.then_inc(c_turned, 1)
                pe.wait_ge(silu_ready, 1)
                pe.wait_ge(wmod_loaded, 16)
                for n in range(3):
                    for k in range(KD):
                        mm(work[n][0:B, :], silu[:, k * B:(k + 1) * B], wmod_sb[:, k, n * 512:(n + 1) * 512],
                           start=(k == 0), stop=(k == KD - 1))
                for n, m in enumerate((0, 1, 2, 3, 6, 7, 8, 9)):
                    for k in range(KD):
                        ins = mm(att[0][:, n * B:(n + 1) * B], wmod_sb[:, k, m * P:(m + 1) * P], silu[:, k * B:(k + 1) * B],
                                 start=(k == 0), stop=(k == KD - 1))
                ins.then_inc(mod_done, 1)
                pe.wait_ge(mod_col_ready, 1)
                pe.wait_ge(wqkv_loaded, 16)
                for g in range(2):
                    for k in range(KD):
                        mm(tr[g][0:B, :], mod_col[:, k, :], wqkv_sb[:, k, g * HD:(g + 1) * HD],
                           start=(k == 0), stop=(k == KD - 1))
                for p in range(NP):
                    for k in range(KD):
                        ins = mm(att[1][:, p * B:(p + 1) * B], wqkv_sb[:, k, QK + p * P:QK + (p + 1) * P], mod_col[:, k, :],
                                 start=(k == 0), stop=(k == KD - 1))
                ins.then_inc(bias_done, 1)
                for g, dst in enumerate((gram, att[0])):
                    for n in range(2):
                        p = 2 * g + n
                        for k in range(KD):
                            ins = nc.tensor.transpose(dst[:, n * D + k * P:n * D + (k + 1) * P],
                                                      wqkv_sb[:, k, QK + p * P:QK + (p + 1) * P], ident[:])
                    ins.then_inc(w_turned, 1)
                pe.wait_ge(ffn_loaded, 48)
                pe.wait_ge(row8_ready, 1)
                for n in range(3):
                    for ch in range(KD):
                        for dh in range(KD):
                            ins = nc.tensor.transpose(work[n][:, ch * D + dh * P:ch * D + (dh + 1) * P],
                                                      w_ffn[:, n, dh, ch * P:(ch + 1) * P], ident[:])
                    ins.then_inc(w_turned, 1)

            def turn_and_gram(b, j, first=False):
                i = CH * b + j
                pe.wait_ge(z_ready, i + 1)
                if first or j == 1:
                    wait_past(pe, z_t_ready, 2 * i)
                elif j == 0:
                    wait_past(pe, h2_ready, 2 * CH * (b - 1))
                else:
                    pe.wait_ge(h2_ready, 2 * (CH * (b - 1) + j - 1))
                for h in range(KD):
                    for t in range(NT):
                        ins = nc.tensor.transpose(tr[h][:, t * P:(t + 1) * P], z[:, j % 2, t, h * P:(h + 1) * P], ident[:])
                    ins.then_inc(z_turned, 1)
                if j == 0 and not first:
                    pe.wait_ge(m_ready, b)
                for t in range(NT):
                    for k in range(KD):
                        ins = mm(gram[:, k * D:(k + 1) * D - k * P], z[:, j % 2, t, k * P:(k + 1) * P], z[:, j % 2, t, k * P:D],
                                 start=(j == 0 and t == 0 and k == 0), stop=(j == CH - 1 and t == NT - 1),
                                 skip_group_check=True)
                ins.then_inc(z_used, 1)

            def attention(b, j):
                i = CH * b + j
                pe.wait_ge(m_ready, b + 1)
                pe.wait_ge(z_t_ready, 2 * i + 2)
                wait_past(pe, t_done, i)
                for q in range(2):
                    for t in (2 * q, 2 * q + 1):
                        for k in range(KD):
                            ins = mm(att[q][:, (t % 2) * D:(t % 2 + 1) * D], z_t[:, j, k, t * P:(t + 1) * P], m_sb[:, k],
                                     start=(k == 0), stop=(k == KD - 1))
                    ins.then_inc(att_done, 1)

            def turn_z2(b, j, last):
                i = CH * b + j
                pe.wait_ge(z2_ready, i + 1)
                if not last and j < CH - 1:
                    pe.wait_ge(z_t_ready, 2 * (i + 1 + CH) + 2)
                else:
                    wait_past(pe, h2_ready, 2 * i)
                for h in range(KD):
                    for t in range(NT):
                        ins = nc.tensor.transpose(tr[h][:, t * P:(t + 1) * P], z2[:, t, h * P:(h + 1) * P], ident[:])
                    ins.then_inc(z2_turned, 1)

            def ffn_in(b, j):
                i = CH * b + j
                pe.wait_ge(xk_ready, i + 1)
                wait_past(pe, th_ready, 2 * i)
                for dh in range(KD):
                    if dh == 1:
                        wait_past(pe, ro_ready, 2 * i - 1)
                    for ch in range(KD):
                        ins = mm(work[dh][:], w_ffn_t[:, 1, ch, dh * P:(dh + 1) * P], xk[:, ch], start=(ch == 0), stop=(ch == KD - 1))
                    ins.then_inc(k_done, 1)
                pe.wait_ge(xr_ready, i + 1)
                for q in range(2):
                    if q == 0:
                        wait_past(pe, ro_ready, 2 * i)
                    else:
                        pe.wait_ge(k_pos_ready, 2 * i + 1)
                    for t in (2 * q, 2 * q + 1):
                        for ch in range(KD):
                            ins = mm(work[2 - 2 * q][:, (t % 2) * D:(t % 2 + 1) * D], xr[:, ch, t * P:(t + 1) * P],
                                     w_ffn_t[:, 0, ch], start=(ch == 0), stop=(ch == KD - 1))
                    ins.then_inc(r_done, 1)

            def ffn_out(b, j):
                i = CH * b + j
                pe.wait_ge(now_ready, b + 1)
                pe.wait_ge(k_act_ready, i + 1)
                for q in range(2):
                    if q == 1:
                        pe.wait_ge(th_ready, 2 * i + 1)
                    for t in (2 * q, 2 * q + 1):
                        for ch in range(KD):
                            ins = mm(work[1 + q][:, (t % 2) * D:(t % 2 + 1) * D], k_act[:, ch, t * P:(t + 1) * P], wvf[:, ch],
                                     start=(ch == 0), stop=(ch == KD - 1))
                    ins.then_inc(o_done, 1)

            def turn_gram(b):
                pe.wait_ge(g_up_ready, b + 1)
                nc.tensor.transpose(gram[:, D + P:2 * D], g_sb[:, 0, P:D], ident[:]).then_inc(gram_turned, 1)

            def gram_q(b):
                pe.wait_ge(g_ready, b + 1)
                pe.wait_ge(qk_ready, b + 1)
                pe.wait_ge(edge_loaded, 32 * (b + 1))
                wait_past(pe, t_done, CH * b)
                for m in range(KD):
                    for k in range(KD):
                        ins = mm(att[m][:], g_sb[:, k, m * P:(m + 1) * P], wqk_aug[:, k, 0:HD], start=(k == 0), stop=(k == KD - 1))
                    ins.then_inc(gq_done, 1)

            def scores(b):
                pe.wait_ge(gq_ready, 2 * b + 2)
                for p in range(NP):
                    for m in range(KD):
                        ins = mm(gram[:, p * P:(p + 1) * P], gq[:, m, p * P:(p + 1) * P], wqk_aug[:, m, HD + p * P:HD + (p + 1) * P],
                                 start=(m == 0), stop=(m == KD - 1))
                ins.then_inc(score_done, 1)

            def wv_attn(b):
                pe.wait_ge(attn_ready, b + 1)
                pe.wait_ge(wv_ready, b + 1)
                for p in range(NP):
                    ins = mm(att[p // 2][:, (p % 2) * D:(p % 2 + 1) * D], attn[:, p], wv_aug[:, p], start=True, stop=True)
                    if p % 2:
                        ins.then_inc(pv_done, 1)

            def make_m(b):
                pe.wait_ge(pv_ready, 2 * b + 2)
                for k in range(KD):
                    for p in range(NP):
                        ins = mm(gram[:, k * D:(k + 1) * D], pv_t[:, p, k * P:(k + 1) * P], wfc_c[:, p], start=(p == 0), stop=(p == NP - 1))
                ins.then_inc(m_done, 1)

            def row_steps(b, last):
                n = b + 1
                for j in range(CH):
                    attention(b, j)
                    if not last:
                        turn_and_gram(n, j)
                    if j > 1:
                        ffn_in(b, j - 2)
                    if not last and j == CH - 1:
                        turn_gram(n)
                    if j:
                        turn_z2(b, j - 1, last)
                    if j > 1:
                        ffn_out(b, j - 2)
                if not last:
                    gram_q(n)
                ffn_in(b, CH - 2)
                if not last:
                    scores(n)
                turn_z2(b, CH - 1, last)
                ffn_out(b, CH - 2)
                if not last:
                    wv_attn(n)
                ffn_in(b, CH - 1)
                if not last:
                    make_m(n)
                ffn_out(b, CH - 1)

            setup()
            pe.wait_ge(w_copied, 5)
            for j in range(CH):
                turn_and_gram(0, j, first=True)
            turn_gram(0)
            gram_q(0)
            scores(0)
            wv_attn(0)
            pe.wait_ge(fc_ready, 1)
            make_m(0)
            row_steps(0, False)
            with pe.Fori(1, B - 1) as b:
                row_steps(b, False)
            row_steps(B - 1, True)


_INS = ['L0_attn_x', 'L0_attn_w_qkv', 'L0_attn_b_qkv', 'L0_attn_w_fc', 'L0_attn_b_fc', 'L0_attn_gamma', 'L0_attn_beta',
        'L0_ffn_W_r', 'L0_ffn_W_k', 'L0_ffn_W_v', 'L0_ffn_mu_r', 'L0_ffn_mu_k', 'L0_c', 'L0_wmod']


def kernel(**inputs):
    import numpy as _np
    import concourse.bacc as _bacc
    from concourse import mybir as _mybir
    from concourse.bass_utils import run_bass_kernel_spmd as _run

    nc = _bacc.Bacc("TRN2", target_bir_lowering=False, num_devices=1)
    arrays, args = {}, []
    for name in _INS:
        a = _np.ascontiguousarray(inputs[name])
        arrays[f"in_{name}_dram"] = a
        args.append(nc.dram_tensor(f"in_{name}_dram", a.shape, _mybir.dt.from_np(a.dtype), kind="ExternalInput").ap())
    shape = arrays["in_L0_attn_x_dram"].shape
    args.append(nc.dram_tensor("out_0_dram", shape, _mybir.dt.float32, kind="ExternalOutput").ap())
    adaln_block(nc, *args)
    r = _run(nc, [arrays], core_ids=[0])
    return r.results[0]["out_0_dram"]
```

```python
from contextlib import ExitStack

import concourse.bass as bass
from concourse import mybir

F32 = mybir.dt.float32
F32R = mybir.dt.float32r
ALU = mybir.AluOpType
ACT = mybir.ActivationFunctionType
AX = mybir.AxisListType.X

P = 128


def adaln_block(nc, x, w_qkv, b_qkv, w_fc, b_fc, gamma, beta, w_r, w_k, w_v, mu_r, mu_k, c, wmod, out):
    B, L, D = x.shape
    HD = w_fc.shape[0]
    DX = 64
    H = HD // DX
    KD = D // P
    NP = H // 2
    CT = 512
    CH = L // CT
    NT = CT // P
    LAST = D - 1
    QK = 2 * HD
    SM_SCALE = float(DX) ** -0.5
    EPS_LN, EPS_ATT = 1e-5, 1e-6
    assert (KD, NP, NT, CH) == (2, 4, 4, 4)

    x_v = x.rearrange("b (j t p) d -> b j p t d", p=P, t=NT)
    out_v = out.rearrange("b (j t p) d -> b j p t d", p=P, t=NT)

    with ExitStack() as ctx:
        def sb(name, shape):
            return ctx.enter_context(nc.sbuf_tensor(name, shape, F32))

        def part(name, shape):
            return ctx.enter_context(nc.sbuf_tensor(name, shape, F32R))

        def bank(name):
            return ctx.enter_context(nc.psum_tensor(name, [P, 512], F32))

        def sem(name):
            return ctx.enter_context(nc.semaphore(name))

        gram = bank("gram")
        tr = [bank(f"tr{h}") for h in range(KD)]
        att = [bank(f"att{q}") for q in range(2)]
        work = [bank(f"work{w}") for w in range(3)]

        def r_banks(alone):
            return (att[0], att[1]) if alone else (work[2], work[0])

        def k_banks(alone):
            return (gram, work[2]) if alone else (work[1], work[2])

        def att_banks(j, alone):
            return tr if alone and j == 1 else att

        ident = sb("ident", [P, P])
        ident_c = sb("ident_c", [P, KD, D])
        last_c = sb("last_c", [P, D])
        neg_half, half, quarter, minus_one, eps_att = (
            sb(n, [P, NT]) for n in ("neg_half", "half", "quarter", "minus_one", "eps_att"))
        wqkv_sb = sb("wqkv_sb", [P, KD, 3 * HD])
        wqk_last = sb("wqk_last", [P, QK])
        bv_col = sb("bv_col", [P, NP])
        wfc_c = sb("wfc_c", [P, NP, D])
        w_rk_hi = part("w_rk_hi", [P, 2, KD, D])
        w_rk_lo = part("w_rk_lo", [P, 2, KD, D])
        w_v_t = sb("w_v_t", [P, KD, D])
        mu_col = sb("mu_col", [P, 2, KD])
        wv_t = sb("wv_t", [P, NP, D])

        th_c = sb("th_c", [P, KD * B])
        silu_u = sb("silu_u", [P, KD * B])
        silu = sb("silu", [P, KD * B])
        mod_col = sb("mod_col", [P, 8, B])
        vb_col = sb("vb_col", [P, NP, B])
        col8 = sb("col8", [B, 2])
        fc_mean = sb("fc_mean", [P, NP])
        scratch = nc.dram_tensor("row_scratch", [B, 5 * D + QK], F32)

        rows = sb("rows", [P, 4, D])
        g_row = sb("g_row", [P, D])
        mod_now = sb("mod_now", [P, 4])
        wvf_hi = part("wvf_hi", [P, KD, D])
        wvf_lo = part("wvf_lo", [P, KD, D])
        d_now = sb("d_now", [P, KD])
        neg_d = sb("neg_d", [P, 1])
        wqk_aug = sb("wqk_aug", [P, KD, QK])
        wv_aug = sb("wv_aug", [P, NP, D])
        res = sb("res", [P, KD, D])
        g_sb = sb("g_sb", [P, KD, D])
        gq = sb("gq", [P, KD, HD])
        s_max = sb("s_max", [P, NP])
        s_dif = sb("s_dif", [P, NP, DX])
        s_exp = sb("s_exp", [P, NP, DX])
        s_sum = sb("s_sum", [P, NP])
        s_inv = sb("s_inv", [P, NP])
        attn = sb("attn", [P, NP, P])
        m_sb = sb("m_sb", [P, KD, D])

        x_in = sb("x_in", [P, CH, NT, D])
        xb = sb("xb", [P, CH, NT, D])
        z = sb("z", [P, 2, NT, D])
        z_t = sb("z_t", [P, CH, KD, CT])
        st_a = sb("st_a", [P, CH, NT, 6])
        ag_a = sb("ag_a", [P, CH, 8, NT])
        ssq = sb("ssq", [P, 2, NT])
        ve_o = sb("ve_o", [P, 2, NT])
        rs_o = sb("rs_o", [P, 2, NT])
        t_buf = sb("t_buf", [P, NT, D])
        x2 = sb("x2", [P, CH, NT, D])
        st_2 = sb("st_2", [P, 2, NT, 6])
        ag_2 = sb("ag_2", [P, 2, 8, NT])
        z2 = sb("z2", [P, NT, D])
        h2t = sb("h2t", [P, KD, 1 + L])
        xr = sb("xr", [P, KD, CT])
        xk_hi, xk_lo, xr_hi, xr_lo, k_hi, k_lo = (
            part(n, [P, KD, CT]) for n in ("xk_hi", "xk_lo", "xr_hi", "xr_lo", "k_hi", "k_lo"))
        y = sb("y", [P, 2, NT, D])

        dif = t_buf[:].rearrange("p t d -> p (t d)").rearrange("p (k n) -> p k n", k=KD)

        xk = wqkv_sb[:, :, QK:3 * HD]
        pv_t = gq[:].rearrange("p m (n d) -> p (m n) d", d=D)

        def y_buf(j, alone):
            return x_in[:, j] if alone else y[:, j % 2]

        def k_split(j, alone):
            return (xr_hi, xr_lo) if alone and j == CH - 1 else (k_hi, k_lo)

        def o_banks(j, alone):
            return att if alone and j == CH - 1 else work[0:2]

        def mixed(j, alone):
            return (z_t[:, 2 * j - CH], z_t[:, 2 * j - CH + 1]) if alone and j >= CH // 2 else (xr[:], xk)

        wmod_sb = x2[:, 0:3].rearrange("p j t d -> p (j t d)").rearrange("p (k n) -> p k n", k=KD)
        w_ffn = y[:].rearrange("p s t d -> p (s t d)")[:, 0:3 * KD * D].rearrange(
            "p (n k d) -> p n k d", n=3, k=KD)
        NR = 5 * D + QK
        CB, CA, QB, GB = 0, D, 2 * D, 2 * D + QK
        room8 = xb[0:B].rearrange("p j t d -> p (j t d)")
        row8 = room8[:, 0:NR]
        tmp8 = room8[:, NR:NR + 4 * D].rearrange("p (n d) -> p n d", n=4)
        bqk8 = z2[0:B].rearrange("p t d -> p (t d)")
        c_sb, gamma8, beta8, bfc8 = (t_buf[0:B, n] for n in range(4))

        ident_ready = sem("ident_ready")
        const_ready = sem("const_ready")
        pool_step = sem("pool_step")
        c_loaded = sem("c_loaded")
        wmod_a_loaded = sem("wmod_a_loaded")
        wmod_b_loaded = sem("wmod_b_loaded")
        wqkv_loaded = sem("wqkv_loaded")
        bias_loaded = sem("bias_loaded")
        small_loaded = sem("small_loaded")
        wfc_loaded = sem("wfc_loaded")
        ffn_loaded = sem("ffn_loaded")
        c_turned = sem("c_turned")
        c_tanh = sem("c_tanh")
        silu_ready = sem("silu_ready")
        mod_a_done = sem("mod_a_done")
        mod_b_done = sem("mod_b_done")
        mod_col_ready = sem("mod_col_ready")
        bias_done = sem("bias_done")
        row8_step = sem("row8_step")
        row8_a_read = sem("row8_a_read")
        row8_a_ready = sem("row8_a_ready")
        row8_b_ready = sem("row8_b_ready")
        vb_ready = sem("vb_ready")
        fc_step = sem("fc_step")
        fc_ready = sem("fc_ready")
        w_turned = sem("w_turned")
        w_copied = sem("w_copied")
        w_split = sem("w_split")
        row8_stored = sem("row8_stored")
        gates_loaded = sem("gates_loaded")
        ca_loaded = sem("ca_loaded")
        gb_loaded = sem("gb_loaded")
        edge_loaded = sem("edge_loaded")
        now_ready = sem("now_ready")
        now_step = sem("now_step")
        prep_step = sem("prep_step")
        prep_base = sem("prep_base")
        qk_ready = sem("qk_ready")
        wv_step = sem("wv_step")
        wv_ready = sem("wv_ready")
        g_up_ready = sem("g_up_ready")
        gram_turned = sem("gram_turned")
        g_ready = sem("g_ready")
        gq_done = sem("gq_done")
        gq_ready = sem("gq_ready")
        score_done = sem("score_done")
        sm_step = sem("sm_step")
        s_dif_ready = sem("s_dif_ready")
        exp_done = sem("exp_done")
        attn_ready = sem("attn_ready")
        pv_done = sem("pv_done")
        pv_ready = sem("pv_ready")
        m_done = sem("m_done")
        m_ready = sem("m_ready")
        x_loaded = [sem(f"x_loaded{j}") for j in range(CH)]
        st_a_done = sem("st_a_done")
        ag_a_step = sem("ag_a_step")
        rs_a_ready = sem("rs_a_ready")
        z_ready = sem("z_ready")
        z_turned = sem("z_turned")
        z_used = sem("z_used")
        z_t_ready = sem("z_t_ready")
        xb_ready = sem("xb_ready")
        att_done = sem("att_done")
        ssq_ready = sem("ssq_ready")
        ve_o_done = sem("ve_o_done")
        rs_o_ready = sem("rs_o_ready")
        t_done = sem("t_done")
        x2_ready = sem("x2_ready")
        st_2_done = sem("st_2_done")
        ag_2_step = sem("ag_2_step")
        rs_2_step = sem("rs_2_step")
        rs_2_ready = sem("rs_2_ready")
        z2_ready = sem("z2_ready")
        z2_turned = sem("z2_turned")
        h2_ready = sem("h2_ready")
        dif_done = sem("dif_done")
        xk_mixed = sem("xk_mixed")
        xr_mixed = sem("xr_mixed")
        xk_hi_ready = sem("xk_hi_ready")
        xr_hi_ready = sem("xr_hi_ready")
        xk_lo_ready = sem("xk_lo_ready")
        xr_lo_ready = sem("xr_lo_ready")
        k_done = sem("k_done")
        k_pos_ready = sem("k_pos_ready")
        k_sq_ready = sem("k_sq_ready")
        k_hi_ready = sem("k_hi_ready")
        k_lo_ready = sem("k_lo_ready")
        r_done = sem("r_done")
        th_ready = sem("th_ready")
        o_done = sem("o_done")
        ro_ready = sem("ro_ready")
        y_ready = sem("y_ready")
        y_end_stored = sem("y_end_stored")
        y_end_ready = sem("y_end_ready")
        y_stored = [sem(f"y_stored{s}") for s in range(2)]

        def wait_past(eng, semaphore, count):
            if not isinstance(count, int) or count > 0:
                eng.wait_ge(semaphore, count)

        block = ctx.enter_context(nc.Block())

        @block.sync
        def _(sp):
            def load_x(b, j):
                sp.dma_start(x_in[:, j], x_v[b, j]).then_inc(x_loaded[j], 16)

            def load_ca(b):
                src = scratch[b, CA:CA + D].partition_broadcast(P)
                sp.dma_start(rows[:, 3], src).then_inc(ca_loaded, 16)
                sp.dma_start(wqk_aug[P - 1:P, KD - 1, :], scratch[b, QB:QB + QK].unsqueeze(0)).then_inc(edge_loaded, 16)
                sp.dma_start(res[P - 1:P, KD - 1, :], scratch[b, CB:CB + D].unsqueeze(0)).then_inc(edge_loaded, 16)

            def load_gates(b):
                src = scratch[b, GB:GB + 2 * D].partition_broadcast(P)
                sp.dma_start(rows[:, 0:2].rearrange("p r d -> p (r d)"), src).then_inc(gates_loaded, 16)

            def load_gb(b):
                src = scratch[b, GB + 2 * D:NR].partition_broadcast(P)
                sp.dma_start(rows[:, 2], src).then_inc(gb_loaded, 16)

            def next_x(b, j):
                sp.wait_ge(z_ready, CH * (b - 1) + j + 1)
                sp.wait_ge(xb_ready, CH * (b - 1) + j + 1)
                load_x(b, j)

            def next_ca(b):
                sp.wait_ge(m_ready, b)
                sp.wait_ge(wv_ready, b)
                load_ca(b)

            def next_gates(b):
                sp.wait_ge(xb_ready, CH * b)
                sp.wait_ge(now_step, 3 * b - 2)
                load_gates(b)

            def next_gb(b):
                sp.wait_ge(now_ready, b)
                load_gb(b)

            def store_y(b, j, alone=False):
                sp.wait_ge(y_ready, CH * b + j + 1)
                sp.dma_start(out_v[b, j], y_buf(j, alone)).then_inc(y_stored[j % 2], 16)

            def row_steps(b, first):
                next_gates(b + 1)
                if not first:
                    store_y(b - 1, 2)
                next_x(b + 2, 0)
                next_x(b + 2, 1)
                if not first:
                    store_y(b - 1, 3)
                next_gb(b + 1)
                next_x(b + 2, 2)
                next_x(b + 2, 3)
                store_y(b, 0)
                store_y(b, 1)
                next_ca(b + 2)

            wmod_v = wmod.rearrange("(k p) n -> p k n", p=P)
            sp.dma_start(c_sb, c).then_inc(c_loaded, 16)
            load_x(0, 0)
            sp.dma_start(wmod_sb[:, :, 0:2 * D], wmod_v[:, :, 0:2 * D]).then_inc(wmod_a_loaded, 16)
            load_x(0, 1)
            load_x(0, 2)
            sp.dma_start(wmod_sb[:, :, 2 * D:6 * D], wmod_v[:, :, 2 * D:6 * D]).then_inc(wmod_b_loaded, 16)
            load_x(0, 3)
            for n, w in enumerate((w_r, w_k, w_v)):
                sp.dma_start(w_ffn[:, n], w.rearrange("(k p) n -> p k n", p=P)).then_inc(ffn_loaded, 16)
            sp.wait_ge(row8_a_ready, 1)
            sp.dma_start(scratch[:, 0:GB], row8[:, 0:GB]).then_inc(row8_stored, 16)
            sp.wait_ge(row8_stored, 16)
            load_ca(0)
            sp.wait_ge(row8_b_ready, 1)
            sp.dma_start(scratch[:, GB:NR], row8[:, GB:NR]).then_inc(row8_stored, 16)
            sp.wait_ge(row8_stored, 32)
            load_gates(0)
            load_gb(0)
            for j in range(CH):
                next_x(1, j)
            next_ca(1)
            row_steps(0, True)
            with sp.Fori(1, B - 2) as b:
                row_steps(b, False)
            next_gates(B - 1)
            store_y(B - 3, 2)
            store_y(B - 3, 3)
            next_gb(B - 1)
            for b in (B - 2, B - 1):
                for j in range(CH):
                    if b < B - 1 or j < CH - 1:
                        store_y(b, j, alone=(b == B - 1 and j > 0))
            for q in range(2):
                half = slice(2 * q, 2 * q + 2)
                sp.wait_ge(y_end_ready, q + 1)
                sp.dma_start(out_v[B - 1, CH - 1, :, half], y_buf(CH - 1, True)[:, half]).then_inc(y_end_stored, 16)
            sp.wait_ge(y_stored[0], 16 * B * CH // 2)
            sp.wait_ge(y_stored[1], 16 * (B * CH // 2 - 1))
            sp.wait_ge(y_end_stored, 32)

        @block.gpsimd
        def _(pool):
            def build_constants():
                nc.gpsimd.memset(ident[:], 0.0).then_inc(pool_step, 1)
                nc.gpsimd.memset(ident_c[:], -1.0 / D).then_inc(pool_step, 1)
                nc.gpsimd.memset(last_c[:], -1.0 / D).then_inc(pool_step, 1)
                pool.wait_ge(pool_step, 3)
                nc.gpsimd.affine_select(out=ident[:], in_=ident[:], compare_op=ALU.not_equal, fill=1.0, base=0,
                                        pattern=[[-1, P]], channel_multiplier=1).then_inc(ident_ready, 1)
                nc.gpsimd.affine_select(out=ident_c[:], in_=ident_c[:], compare_op=ALU.not_equal, fill=1.0 - 1.0 / D,
                                        base=0, pattern=[[P, KD], [-1, D]], channel_multiplier=1).then_inc(const_ready, 1)
                nc.gpsimd.memset(last_c[:, LAST:D], 1.0 - 1.0 / D).then_inc(const_ready, 1)
                nc.gpsimd.memset(half[:], 0.5).then_inc(const_ready, 1)
                nc.gpsimd.memset(minus_one[:], -1.0).then_inc(const_ready, 1)
                nc.gpsimd.memset(quarter[:], 0.25).then_inc(const_ready, 1)
                nc.gpsimd.memset(eps_att[:], EPS_ATT).then_inc(const_ready, 1)
                nc.gpsimd.memset(neg_half[:], -0.5).then_inc(const_ready, 1)
                nc.gpsimd.memset(attn[:], 0.0).then_inc(const_ready, 1)
                nc.gpsimd.memset(h2t[:, :, 0:1], 0.0).then_inc(const_ready, 1)
                nc.gpsimd.memset(z[:, :, :, LAST:D], 1.0).then_inc(const_ready, 1)
                pool.wait_ge(const_ready, 10)

            def layernorm_factors(i, st, ag, st_done, ag_step, ready, eps):
                pool.wait_ge(st_done, i + 1)
                nc.gpsimd.tensor_tensor(ag[:, 0], st[:, :, 1], st[:, :, 4], ALU.add)
                nc.gpsimd.tensor_tensor(ag[:, 1], st[:, :, 1], st[:, :, 4], ALU.subtract)
                nc.gpsimd.tensor_tensor(ag[:, 2], st[:, :, 2], st[:, :, 5], ALU.add).then_inc(ag_step, 1)
                pool.wait_ge(ag_step, 4 * i + 1)
                nc.gpsimd.tensor_tensor(ag[:, 3], ag[:, 0], half[:], ALU.mult)
                nc.gpsimd.tensor_tensor(ag[:, 4], ag[:, 1], ag[:, 1], ALU.mult)
                nc.gpsimd.tensor_scalar(ag[:, 5], ag[:, 2], 1.0 / D, eps, ALU.mult, ALU.add).then_inc(ag_step, 1)
                pool.wait_ge(ag_step, 4 * i + 2)
                nc.gpsimd.tensor_tensor(ag[:, 4], ag[:, 4], quarter[:], ALU.mult).then_inc(ag_step, 1)
                pool.wait_ge(ag_step, 4 * i + 3)
                nc.gpsimd.tensor_tensor(ag[:, 6], ag[:, 4], ag[:, 5], ALU.add).then_inc(ag_step, 1)
                pool.wait_ge(ag_step, 4 * i + 4)
                nc.gpsimd.tensor_tensor(ag[:, 7], ag[:, 6], neg_half[:], ALU.pow).then_inc(ready, 1)

            def rstd_a(b, j):
                layernorm_factors(CH * b + j, st_a[:, j], ag_a[:, j], st_a_done, ag_a_step, rs_a_ready, EPS_LN)

            def rstd_2(b, j):
                i, ag = CH * b + j, ag_2[:, j % 2]
                layernorm_factors(i, st_2[:, j % 2], ag, st_2_done, ag_2_step, rs_2_step, EPS_LN)
                nc.gpsimd.tensor_tensor(ag[:, 0], ag[:, 3], minus_one[:], ALU.mult).then_inc(rs_2_step, 1)
                pool.wait_ge(rs_2_step, 2 * i + 2)
                nc.gpsimd.tensor_tensor(ag[:, 1], ag[:, 0], ag[:, 7], ALU.mult).then_inc(rs_2_ready, 1)

            def rstd_o(b, j):
                i, s = CH * b + j, j % 2
                pool.wait_ge(ssq_ready, i + 1)
                nc.gpsimd.tensor_tensor(ve_o[:, s], ssq[:, s], eps_att[:], ALU.add).then_inc(ve_o_done, 1)
                pool.wait_ge(ve_o_done, i + 1)
                nc.gpsimd.tensor_tensor(rs_o[:, s], ve_o[:, s], neg_half[:], ALU.pow).then_inc(rs_o_ready, 1)

            def make_xb(b, j, first=False):
                pool.wait_ge(x_loaded[j], 16 * (b + 1))
                pool.wait_ge(gates_loaded, 16 * (b + 1))
                if not first:
                    pool.wait_ge(x2_ready, CH * (b - 1) + j + 1)
                nc.gpsimd.tensor_tensor(xb[:, j], x_in[:, j], rows[:, 1].unsqueeze(1).to_broadcast([P, NT, D]),
                                        ALU.add).then_inc(xb_ready, 1)

            def prep_wv(b):
                pool.wait_ge(ca_loaded, 16 * (b + 1))
                wait_past(pool, m_ready, b)
                nc.gpsimd.tensor_tensor(wv_aug[:], wv_t[:], rows[:, 3].unsqueeze(1).to_broadcast([P, NP, D]),
                                        ALU.mult).then_inc(wv_step, 1)
                pool.wait_ge(wv_step, 2 * b + 1)
                nc.gpsimd.tensor_tensor(wv_aug[:, :, 0:LAST], wv_aug[:, :, 0:LAST],
                                        wv_aug[:, :, LAST:D].to_broadcast([P, NP, LAST]), ALU.subtract).then_inc(wv_step, 1)
                pool.wait_ge(wv_step, 2 * b + 2)
                nc.gpsimd.tensor_copy(wv_aug[:, :, LAST], vb_col[:, :, b]).then_inc(wv_ready, 1)

            def low_xk(b, j, alone=False):
                i = CH * b + j
                pool.wait_ge(xk_hi_ready, i + 1)
                nc.gpsimd.tensor_tensor(xk_lo[:], mixed(j, alone)[1], xk_hi[:].bitcast(F32), ALU.subtract).then_inc(xk_lo_ready, 1)

            def add_y(b, j, alone=False):
                i, y_j = CH * b + j, y_buf(j, alone)
                pool.wait_ge(ro_ready, 2 * i + 2)
                nc.gpsimd.tensor_tensor(y_j, y_j, x2[:, j], ALU.add).then_inc(y_ready, 1)

            def row_steps(b, first, far):
                n = b + 1
                rstd_o(b, 0)
                if not first:
                    low_xk(b - 1, 3)
                    add_y(b - 1, 2)
                rstd_2(b, 0)
                if first:
                    rstd_o(b, 1)
                    rstd_a(n, 2)
                    rstd_2(b, 1)
                    low_xk(b, 0)
                    rstd_o(b, 2)
                    rstd_a(n, 3)
                    make_xb(n, 0)
                else:
                    prep_wv(n)
                    rstd_o(b, 1)
                    make_xb(n, 0)
                    rstd_2(b, 1)
                    make_xb(n, 1)
                    low_xk(b, 0)
                    rstd_o(b, 2)
                    add_y(b - 1, 3)
                rstd_2(b, 2)
                if first:
                    make_xb(n, 1)
                make_xb(n, 2)
                rstd_o(b, 3)
                low_xk(b, 1)
                if first:
                    prep_wv(n)
                add_y(b, 0)
                make_xb(n, 3)
                rstd_2(b, 3)
                low_xk(b, 2)
                if far:
                    rstd_a(n + 1, 0)
                    rstd_a(n + 1, 1)
                add_y(b, 1)
                if far:
                    rstd_a(n + 1, 2)
                    rstd_a(n + 1, 3)

            def last_row(b):
                rstd_o(b, 0)
                low_xk(b - 1, 3)
                rstd_o(b, 1)
                rstd_2(b, 0)
                add_y(b - 1, 2)
                rstd_o(b, 2)
                rstd_2(b, 1)
                low_xk(b, 0)
                rstd_o(b, 3)
                rstd_2(b, 2)
                add_y(b - 1, 3)
                low_xk(b, 1)
                rstd_2(b, 3)
                low_xk(b, 2, alone=True)
                add_y(b, 0)
                low_xk(b, 3, alone=True)
                for j in range(1, CH - 1):
                    add_y(b, j, alone=True)

            build_constants()
            for j in range(CH):
                rstd_a(0, j)
            pool.wait_ge(w_copied, 2)
            pool.wait_ge(vb_ready, 1)
            prep_wv(0)
            for j in range(CH):
                make_xb(0, j, first=True)
            rstd_a(1, 0)
            rstd_a(1, 1)
            row_steps(0, True, True)
            with pool.Fori(1, B - 2) as b:
                row_steps(b, False, True)
            row_steps(B - 2, False, False)
            last_row(B - 1)

        @block.scalar
        def _(act):
            def load_weights():
                act.dma_start(bqk8, b_qkv[0:QK].partition_broadcast(B)).then_inc(bias_loaded, 16)
                act.dma_start(bfc8, b_fc.partition_broadcast(B)).then_inc(bias_loaded, 16)

            def load_more():
                act.dma_start(wqkv_sb[:], w_qkv.rearrange("(k p) n -> p k n", p=P)).then_inc(wqkv_loaded, 16)
                with nc.allow_non_contiguous_dma(reason="three short vectors onto partitions"):
                    act.dma_start(bv_col[:], b_qkv[QK:3 * HD].rearrange("(n p) -> p n", p=P)).then_inc(small_loaded, 16)
                    act.dma_start(mu_col[:, 0], mu_r.rearrange("(k p) -> p k", p=P)).then_inc(small_loaded, 16)
                    act.dma_start(mu_col[:, 1], mu_k.rearrange("(k p) -> p k", p=P)).then_inc(small_loaded, 16)
                act.dma_start(wqk_last[:], w_qkv[LAST, 0:QK].partition_broadcast(P)).then_inc(small_loaded, 16)
                act.dma_start(gamma8, gamma.partition_broadcast(B)).then_inc(small_loaded, 16)
                act.dma_start(beta8, beta.partition_broadcast(B)).then_inc(small_loaded, 16)
                act.dma_start(wfc_c[:], w_fc.rearrange("(n p) d -> p n d", p=P)).then_inc(wfc_loaded, 16)

            def tanh_c():
                act.wait_ge(c_turned, 1)
                nc.scalar.activation(th_c[:], work[0][:, 0:KD * B], ACT.Tanh, scale=0.5).then_inc(c_tanh, 1)

            def copy_weights(first, dsts):
                for n, (dst, src) in enumerate(dsts):
                    act.wait_ge(w_turned, first + n + 1)
                    nc.scalar.activation(dst.rearrange("p a d -> p (a d)"), src[:], ACT.Copy).then_inc(w_copied, 1)

            def copy_z_t(b, j):
                i = CH * b + j
                for h in range(KD):
                    act.wait_ge(z_turned, 2 * i + h + 1)
                    nc.scalar.activation(z_t[:, j, h], tr[h][:], ACT.Copy).then_inc(z_t_ready, 1)

            def copy_gram(b):
                act.wait_ge(z_used, CH * (b + 1))
                nc.scalar.activation(g_sb[:, 0], gram[:, 0:D], ACT.Copy)
                nc.scalar.activation(g_sb[:, 1, P:D], gram[:, D:D + P], ACT.Copy).then_inc(g_up_ready, 1)

            def copy_gram_low(b):
                act.wait_ge(gram_turned, b + 1)
                nc.scalar.activation(g_sb[:, 1, 0:P], gram[:, D + P:2 * D], ACT.Copy).then_inc(g_ready, 1)

            def copy_gq(b):
                for m in range(KD):
                    act.wait_ge(gq_done, 2 * b + m + 1)
                    nc.scalar.activation(gq[:, m], att[m][:], ACT.Copy).then_inc(gq_ready, 1)

            def exps(b):
                act.wait_ge(s_dif_ready, b + 1)
                nc.scalar.activation(s_exp[:], s_dif[:], ACT.Exp, scale=SM_SCALE).then_inc(exp_done, 1)

            def copy_pv(b):
                for g in range(2):
                    act.wait_ge(pv_done, 2 * b + g + 1)
                    nc.scalar.activation(pv_t[:, 2 * g:2 * g + 2].rearrange("p n d -> p (n d)"), att[g][:],
                                         ACT.Copy).then_inc(pv_ready, 1)

            def squares(b, j, alone=False):
                i, s = CH * b + j, j % 2
                if alone:
                    act.wait_ge(xb_ready, i + 1)
                elif j == CH - 1:
                    wait_past(act, y_ready, CH * b)
                sq_out = x_in if alone else x2
                for t in range(NT):
                    if t % 2 == 0:
                        act.wait_ge(att_done, 2 * i + t // 2 + 1)
                    sq = nc.scalar.activation(sq_out[:, j, t], att_banks(j, alone)[t // 2][:, (t % 2) * D:(t % 2 + 1) * D], ACT.Square,
                                              scale=float(D) ** -0.5, accum_out=ssq[:, s, t:t + 1])
                sq.then_inc(ssq_ready, 1)

            def copy_h2(b, j):
                i = CH * b + j
                for h in range(KD):
                    act.wait_ge(z2_turned, 2 * i + h + 1)
                    nc.scalar.activation(h2t[:, h, 1 + j * CT:1 + (j + 1) * CT], tr[h][:], ACT.Identity,
                                         bias=mod_now[:, h:h + 1], scale=mod_now[:, 2 + h:3 + h]).then_inc(h2_ready, 1)

            def split_xr(b, j, alone=False):
                i = CH * b + j
                wait_past(act, r_done, 2 * i)
                act.wait_ge(xr_mixed, i + 1)
                nc.scalar.activation(xr_hi[:], mixed(j, alone)[0], ACT.Copy).then_inc(xr_hi_ready, 1)

            def split_xk(b, j, alone=False):
                i = CH * b + j
                wait_past(act, k_done, 2 * i)
                act.wait_ge(xk_mixed, i + 1)
                nc.scalar.activation(xk_hi[:], mixed(j, alone)[1], ACT.Copy).then_inc(xk_hi_ready, 1)

            def take_r(b, j, alone=False):
                i, y_j = CH * b + j, y_buf(j, alone)
                if not alone:
                    wait_past(act, y_stored[j % 2], 16 * (2 * b + j // 2))
                for q in range(2):
                    act.wait_ge(r_done, 2 * i + q + 1)
                    nc.scalar.activation(y_j[:, 2 * q:2 * q + 2].rearrange("p t d -> p (t d)"), r_banks(alone)[q][:],
                                         ACT.Tanh, scale=0.5).then_inc(th_ready, 1)

            def take_k(b, j, alone=False, halves=(0, 1)):
                i = CH * b + j
                for h in halves:
                    k = k_banks(alone)[h]
                    act.wait_ge(k_done, 2 * i + h + 1)
                    nc.scalar.activation(k[:], k[:], ACT.Relu).then_inc(k_pos_ready, 1)
                    act.wait_ge(k_pos_ready, 2 * i + h + 1)
                    nc.scalar.activation(k[:], k[:], ACT.Square).then_inc(k_sq_ready, 1)
                    act.wait_ge(k_sq_ready, 2 * i + h + 1)
                    nc.scalar.activation(k_split(j, alone)[0][:, h], k[:], ACT.Copy).then_inc(k_hi_ready, 1)

            def prep_base_qk(b):
                act.wait_ge(prep_step, 2 * b + 2)
                for k in range(KD):
                    n = P if k < KD - 1 else P - 1
                    nc.scalar.activation(wqk_aug[0:n, k], wqk_last[0:n], ACT.Copy, scale=neg_d[0:n])
                    ins = nc.scalar.activation(res[0:n, k], ident_c[0:n, k], ACT.Copy, scale=d_now[0:n, k:k + 1])
                ins.then_inc(prep_base, 1)

            def make_z2(b, j):
                i, s = CH * b + j, j % 2
                act.wait_ge(rs_2_ready, i + 1)
                for t in range(NT):
                    ins = nc.scalar.activation(z2[:, t], x2[:, j, t], ACT.Identity, bias=ag_2[:, s, 1, t:t + 1],
                                               scale=ag_2[:, s, 7, t:t + 1])
                ins.then_inc(z2_ready, 1)

            def row_steps(b, first):
                n = b + 1
                squares(b, 0)
                copy_z_t(n, 0)
                prep_base_qk(n)
                if first:
                    squares(b, 1)
                    copy_z_t(n, 1)
                    make_z2(b, 0)
                else:
                    take_r(b - 1, 3)
                    take_k(b - 1, 3)
                    make_z2(b, 0)
                    squares(b, 1)
                    copy_z_t(n, 1)
                copy_h2(b, 0)
                split_xr(b, 0)
                split_xk(b, 0)
                squares(b, 2)
                copy_z_t(n, 2)
                take_r(b, 0)
                make_z2(b, 1)
                take_k(b, 0)
                copy_h2(b, 1)
                squares(b, 3)
                make_z2(b, 2)
                copy_z_t(n, 3)
                split_xr(b, 1)
                split_xk(b, 1)
                copy_gram(n)
                copy_gram_low(n)
                copy_h2(b, 2)
                take_r(b, 1)
                take_k(b, 1)
                copy_gq(n)
                split_xr(b, 2)
                split_xk(b, 2)
                make_z2(b, 3)
                exps(n)
                take_r(b, 2)
                take_k(b, 2, halves=(0,))
                copy_pv(n)
                take_k(b, 2, halves=(1,))
                copy_h2(b, 3)
                split_xr(b, 3)
                split_xk(b, 3)

            def last_row(b):
                squares(b, 0)
                squares(b, 1, alone=True)
                take_r(b - 1, 3)
                take_k(b - 1, 3)
                squares(b, 2, alone=True)
                make_z2(b, 0)
                copy_h2(b, 0)
                make_z2(b, 1)
                split_xr(b, 0)
                split_xk(b, 0)
                squares(b, 3, alone=True)
                copy_h2(b, 1)
                take_r(b, 0)
                split_xr(b, 1)
                make_z2(b, 2)
                take_k(b, 0, halves=(0,))
                split_xk(b, 1)
                take_k(b, 0, halves=(1,))
                copy_h2(b, 2)
                take_r(b, 1, alone=True)
                split_xr(b, 2, alone=True)
                make_z2(b, 3)
                take_k(b, 1, alone=True)
                split_xk(b, 2, alone=True)
                copy_h2(b, 3)
                take_r(b, 2, alone=True)
                split_xr(b, 3, alone=True)
                split_xk(b, 3, alone=True)
                take_k(b, 2, alone=True)
                take_r(b, 3, alone=True)
                take_k(b, 3, alone=True)

            load_weights()
            tanh_c()
            load_more()
            copy_z_t(0, 0)
            copy_z_t(0, 1)
            prep_base_qk(0)
            copy_z_t(0, 2)
            copy_weights(0, [(wv_t[:, 0:2], att[0]), (wv_t[:, 2:4], att[1])])
            copy_z_t(0, 3)
            copy_gram(0)
            copy_gram_low(0)
            copy_gq(0)
            exps(0)
            copy_weights(2, [(w_rk_hi[:, 0], work[0]), (w_rk_hi[:, 1], work[1]), (w_v_t[:], work[2])])
            copy_pv(0)
            row_steps(0, True)
            with act.Fori(1, B - 1) as b:
                row_steps(b, False)
            last_row(B - 1)

        @block.vector
        def _(dve):
            def make_silu():
                dve.wait_ge(c_tanh, 1)
                nc.vector.scalar_tensor_tensor(silu_u[:], th_c[:], 1.0, work[0][:, 0:KD * B], ALU.add,
                                               ALU.mult).then_inc(row8_step, 1)
                dve.wait_ge(row8_step, 1)
                nc.vector.tensor_scalar(silu[:], silu_u[:], 0.5, None, ALU.mult).then_inc(silu_ready, 1)

            def take_mod_col(half, done):
                dve.wait_ge(done, 1)
                flat = mod_col[:].rearrange("p m b -> p (m b)")
                w = KD * B
                for m, add in ((2 * half, 0.0), (2 * half + 1, 1.0)):
                    ins = nc.vector.tensor_scalar(flat[:, m * w:(m + 1) * w], att[0][:, m * w:(m + 1) * w], add, None, ALU.add)
                ins.then_inc(mod_col_ready, 1)

            def rows_a():
                centred = row8[:, CB:CB + D]
                dve.wait_ge(bias_loaded, 16 * 2)
                nc.vector.tensor_scalar(row8[:, CA:CA + D], work[0][0:B, D:2 * D], 1.0, None, ALU.add)
                nc.vector.scalar_tensor_tensor(centred, work[0][0:B, 0:D], 0.0, bfc8, ALU.add, ALU.add,
                                               accum_out=col8[:, 0:1]).then_inc(row8_a_read, 1)
                dve.wait_ge(row8_a_read, 1)
                nc.vector.tensor_scalar(col8[:, 1:2], col8[:, 0:1], 1.0 / D, None, ALU.mult).then_inc(row8_step, 1)
                dve.wait_ge(row8_step, 2)
                nc.vector.tensor_scalar(centred, centred, col8[:, 1:2], None,
                                        ALU.subtract).then_inc(row8_step, 1)

            def rows_bias():
                dve.wait_ge(bias_done, 1)
                for g in range(2):
                    ins = nc.vector.tensor_tensor(row8[:, QB + g * HD:QB + (g + 1) * HD], work[1 + g][0:B, :],
                                                  bqk8[:, g * HD:(g + 1) * HD], ALU.add)
                ins.then_inc(row8_a_ready, 1)
                dve.wait_ge(small_loaded, 16 * 6)
                for p in range(NP):
                    ins = nc.vector.tensor_scalar(vb_col[:, p], att[1][:, p * B:(p + 1) * B], bv_col[:, p:p + 1], None, ALU.add)
                ins.then_inc(vb_ready, 1)

            def rows_b():
                steps = 3
                for n in range(2):
                    src, size, sign = work[0][0:B, n * D:(n + 1) * D], tmp8[:, 2 * n], tmp8[:, 2 * n + 1]
                    nc.vector.tensor_scalar(sign, src, -1.0, None, ALU.mult).then_inc(row8_step, 1)
                    dve.wait_ge(row8_step, steps + 1)
                    nc.vector.tensor_tensor(size, sign, src, ALU.max).then_inc(row8_step, 1)
                    dve.wait_ge(row8_step, steps + 2)
                    nc.vector.tensor_scalar(sign, src, 0.0, 2.0, ALU.is_ge, ALU.mult).then_inc(row8_step, 1)
                    nc.vector.tensor_scalar(size, size, 0.25, None, ALU.max).then_inc(row8_step, 1)
                    dve.wait_ge(row8_step, steps + 4)
                    nc.vector.scalar_tensor_tensor(size, sign, -1.0, size, ALU.add, ALU.mult).then_inc(row8_step, 1)
                    dve.wait_ge(row8_step, steps + 5)
                    steps += 5
                nc.vector.tensor_tensor(row8[:, GB:GB + D], tmp8[:, 0], gamma8, ALU.mult)
                nc.vector.tensor_tensor(row8[:, GB + D:GB + 2 * D], tmp8[:, 0], beta8, ALU.mult)
                nc.vector.tensor_scalar(row8[:, GB + 2 * D:NR], tmp8[:, 2], 0.5, None, ALU.mult).then_inc(row8_b_ready, 1)

            def centre_fc():
                dve.wait_ge(wfc_loaded, 16)
                nc.vector.tensor_reduce(fc_mean[:], wfc_c[:], AX, ALU.add).then_inc(fc_step, 1)
                dve.wait_ge(fc_step, 1)
                nc.vector.tensor_scalar(fc_mean[:], fc_mean[:], 1.0 / D, None, ALU.mult).then_inc(fc_step, 1)
                dve.wait_ge(fc_step, 2)
                for p in range(NP):
                    ins = nc.vector.tensor_scalar(wfc_c[:, p], wfc_c[:, p], fc_mean[:, p:p + 1], None, ALU.subtract)
                ins.then_inc(fc_ready, 1)

            def stats_a(b, j):
                i = CH * b + j
                dve.wait_ge(x_loaded[j], 16 * (b + 1))
                for t in range(NT):
                    ins = nc.vector.bn_stats(st_a[:, j, t], x_in[:, j, t])
                ins.then_inc(st_a_done, 1)

            def make_z(b, j, first=False):
                i = CH * b + j
                dve.wait_ge(rs_a_ready, i + 1)
                if not (first and j < 2):
                    dve.wait_ge(z_used, i - 1)
                for t in range(NT):
                    ins = nc.vector.tensor_scalar(z[:, j % 2, t, 0:LAST], x_in[:, j, t, 0:LAST], ag_a[:, j, 3, t:t + 1],
                                                  ag_a[:, j, 7, t:t + 1], ALU.subtract, ALU.mult)
                ins.then_inc(z_ready, 1)

            def make_x2(b, j, mixes=None, alone=False):
                i, s = CH * b + j, j % 2
                wait_past(dve, xk_mixed, CH * b + (max(j - 1, 0) if mixes is None else mixes))
                dve.wait_ge(rs_o_ready, i + 1)
                for t in range(NT):
                    ins = nc.vector.scalar_tensor_tensor(t_buf[:, t], att_banks(j, alone)[t // 2][:, (t % 2) * D:(t % 2 + 1) * D],
                                                         rs_o[:, s, t:t + 1], g_row[:], ALU.mult, ALU.mult)
                ins.then_inc(t_done, 1)
                dve.wait_ge(t_done, i + 1)
                dve.wait_ge(xb_ready, i + 1)
                if alone:
                    dve.wait_ge(y_ready, CH * (b - 1) + j + 1)
                nc.vector.tensor_tensor(x2[:, j], t_buf[:], xb[:, j], ALU.add).then_inc(x2_ready, 1)

            def stats_2(b, j):
                i, s = CH * b + j, j % 2
                dve.wait_ge(x2_ready, i + 1)
                for t in range(NT):
                    ins = nc.vector.bn_stats(st_2[:, s, t], x2[:, j, t])
                ins.then_inc(st_2_done, 1)

            def mix(b, j, made=None, alone=False):
                i = CH * b + j
                if not alone:
                    wait_past(dve, xr_lo_ready, i)
                    wait_past(dve, xk_lo_ready, i)
                dve.wait_ge(x2_ready, CH * b + (min(j + 2, CH) if made is None else made))
                dve.wait_ge(h2_ready, 2 * i + 2)
                prev = h2t[:, :, j * CT:(j + 1) * CT]
                nc.vector.tensor_tensor(dif, h2t[:, :, 1 + j * CT:1 + (j + 1) * CT], prev, ALU.subtract).then_inc(dif_done, 1)
                dve.wait_ge(dif_done, i + 1)
                for n, (dst, ready) in enumerate(zip(mixed(j, alone), (xr_mixed, xk_mixed))):
                    for h in range(KD):
                        ins = nc.vector.scalar_tensor_tensor(dst[:, h], dif[:, h], mu_col[:, n, h:h + 1], prev[:, h],
                                                             ALU.mult, ALU.add)
                    ins.then_inc(ready, 1)

            def low_xr(b, j, alone=False):
                i = CH * b + j
                dve.wait_ge(xr_hi_ready, i + 1)
                nc.vector.tensor_tensor(xr_lo[:], mixed(j, alone)[0], xr_hi[:].bitcast(F32), ALU.subtract).then_inc(xr_lo_ready, 1)

            def low_k(b, j, alone=False):
                i = CH * b + j
                for h in range(KD):
                    dve.wait_ge(k_hi_ready, 2 * i + h + 1)
                    hi, lo = k_split(j, alone)
                    nc.vector.tensor_tensor(lo[:, h], k_banks(alone)[h][:], hi[:, h].bitcast(F32), ALU.subtract).then_inc(k_lo_ready, 1)

            def gate_o(b, j, alone=False, add=False):
                i, y_j = CH * b + j, y_buf(j, alone)
                dve.wait_ge(th_ready, 2 * i + 2)
                for q in range(2):
                    dve.wait_ge(o_done, 2 * i + q + 1)
                    half = y_j[:, 2 * q:2 * q + 2].rearrange("p t d -> p (t d)")
                    nc.vector.scalar_tensor_tensor(half, half, 1.0, o_banks(j, alone)[q][:], ALU.add, ALU.mult).then_inc(ro_ready, 1)
                    if add:
                        dve.wait_ge(ro_ready, 2 * i + q + 1)
                        nc.vector.tensor_tensor(half, half, x2[:, j, 2 * q:2 * q + 2].rearrange("p t d -> p (t d)"),
                                                ALU.add).then_inc(y_end_ready, 1)

            def take_g(b):
                dve.wait_ge(gates_loaded, 16 * (b + 1))
                nc.vector.tensor_copy(g_row[:], rows[:, 0])
                nc.vector.tensor_copy(mod_now[:], mod_col[:, 4:8, b]).then_inc(now_step, 1)
                dve.wait_ge(now_step, 3 * b + 1)

            def take_wvf(b, alone=False):
                if not alone:
                    dve.wait_ge(x2_ready, CH * b + 2)
                    dve.wait_ge(xk_mixed, CH * b + 1)
                wvf = w_v_t[:] if alone else t_buf[:, 0:KD]
                dve.wait_ge(gb_loaded, 16 * (b + 1))
                nc.vector.tensor_tensor(wvf, w_v_t[:], rows[:, 2].unsqueeze(1).to_broadcast([P, KD, D]),
                                        ALU.mult).then_inc(now_step, 1)
                dve.wait_ge(now_step, 3 * b + 2)
                nc.vector.tensor_copy(wvf_hi[:], wvf).then_inc(now_step, 1)
                dve.wait_ge(now_step, 3 * b + 3)
                nc.vector.tensor_tensor(wvf_lo[:], wvf, wvf_hi[:].bitcast(F32), ALU.subtract).then_inc(now_ready, 1)
                dve.wait_ge(now_ready, b + 1)

            def prep_now(b):
                dve.wait_ge(ca_loaded, 16 * (b + 1))
                nc.vector.tensor_scalar(neg_d[:], rows[:, 3, LAST:D], -1.0, None, ALU.mult).then_inc(prep_step, 1)
                nc.vector.tensor_copy(d_now[:], mod_col[:, 2:4, b]).then_inc(prep_step, 1)

            def prep_qk(b):
                dve.wait_ge(prep_base, b + 1)
                for k in range(KD):
                    n = P if k < KD - 1 else P - 1
                    nc.vector.scalar_tensor_tensor(wqk_aug[0:n, k], wqkv_sb[0:n, k, 0:QK], d_now[0:n, k:k + 1],
                                                   wqk_aug[0:n, k], ALU.mult, ALU.add)
                    ins = nc.vector.scalar_tensor_tensor(res[0:n, k], last_c[0:n], neg_d[0:n], res[0:n, k],
                                                         ALU.mult, ALU.add)
                ins.then_inc(qk_ready, 1)

            def split_rk():
                for n in range(2):
                    dve.wait_ge(w_copied, n + 3)
                    ins = nc.vector.tensor_tensor(w_rk_lo[:, n].rearrange("p k d -> p (k d)"), work[n][:],
                                                  w_rk_hi[:, n].rearrange("p k d -> p (k d)").bitcast(F32), ALU.subtract)
                ins.then_inc(w_split, 1)

            def softmax_dif(b):
                dve.wait_ge(score_done, b + 1)
                for g in range(2):
                    lo = g * DX
                    block = gram[lo:lo + DX, :].rearrange("p (n e) -> p n e", n=NP)[:, :, lo:lo + DX]
                    nc.vector.tensor_reduce(s_max[lo:lo + DX], block, AX, ALU.max).then_inc(sm_step, 1)
                dve.wait_ge(sm_step, 4 * b + 2)
                for g in range(2):
                    lo = g * DX
                    block = gram[lo:lo + DX, :].rearrange("p (n e) -> p n e", n=NP)[:, :, lo:lo + DX]
                    ins = nc.vector.tensor_tensor(s_dif[lo:lo + DX], block,
                                                  s_max[lo:lo + DX].unsqueeze(2).to_broadcast([DX, NP, DX]), ALU.subtract)
                ins.then_inc(s_dif_ready, 1)

            def softmax_norm(b):
                dve.wait_ge(exp_done, b + 1)
                nc.vector.tensor_reduce(s_sum[:], s_exp[:], AX, ALU.add).then_inc(sm_step, 1)
                dve.wait_ge(sm_step, 4 * b + 3)
                nc.vector.reciprocal(s_inv[:], s_sum[:]).then_inc(sm_step, 1)
                dve.wait_ge(sm_step, 4 * b + 4)
                for g in range(2):
                    lo = g * DX
                    ins = nc.vector.tensor_tensor(attn[lo:lo + DX, :, lo:lo + DX], s_exp[lo:lo + DX],
                                                  s_inv[lo:lo + DX].unsqueeze(2).to_broadcast([DX, NP, DX]), ALU.mult)
                ins.then_inc(attn_ready, 1)

            def make_m(b):
                dve.wait_ge(m_done, b + 1)
                dve.wait_ge(edge_loaded, 32 * (b + 1))
                nc.vector.tensor_tensor(m_sb[:].rearrange("p k d -> p (k d)"), gram[:],
                                        res[:].rearrange("p k d -> p (k d)"), ALU.add).then_inc(m_ready, 1)

            def row_steps(b, first, far):
                n = b + 1
                take_g(b)
                prep_now(n)
                make_x2(b, 0)
                stats_2(b, 0)
                if first:
                    stats_a(n, 2)
                    stats_a(n, 3)
                    make_x2(b, 1)
                    stats_2(b, 1)
                    make_z(n, 2)
                else:
                    prep_qk(n)
                    low_k(b - 1, 3)
                    make_z(n, 2)
                    make_x2(b, 1)
                    stats_2(b, 1)
                mix(b, 0)
                low_xr(b, 0)
                if first:
                    prep_qk(n)
                else:
                    gate_o(b - 1, 3)
                take_wvf(b)
                make_x2(b, 2)
                stats_2(b, 2)
                low_k(b, 0)
                make_z(n, 3)
                mix(b, 1)
                low_xr(b, 1)
                gate_o(b, 0)
                make_x2(b, 3)
                mix(b, 2)
                low_k(b, 1)
                stats_2(b, 3)
                if far:
                    stats_a(n + 1, 0)
                low_xr(b, 2)
                gate_o(b, 1)
                softmax_dif(n)
                if far:
                    stats_a(n + 1, 1)
                softmax_norm(n)
                if far:
                    make_z(n + 1, 0)
                    make_z(n + 1, 1)
                    stats_a(n + 1, 2)
                low_k(b, 2)
                make_m(n)
                mix(b, 3)
                if far:
                    stats_a(n + 1, 3)
                gate_o(b, 2)
                low_xr(b, 3)

            def last_row(b):
                take_g(b)
                make_x2(b, 0)
                stats_2(b, 0)
                make_x2(b, 1, mixes=0, alone=True)
                stats_2(b, 1)
                low_k(b - 1, 3)
                make_x2(b, 2, mixes=0, alone=True)
                mix(b, 0, made=3)
                low_xr(b, 0)
                gate_o(b - 1, 3)
                stats_2(b, 2)
                mix(b, 1, made=3)
                low_xr(b, 1)
                make_x2(b, 3, mixes=2, alone=True)
                take_wvf(b, alone=True)
                low_k(b, 0)
                stats_2(b, 3)
                mix(b, 2, alone=True)
                low_xr(b, 2, alone=True)
                gate_o(b, 0)
                low_k(b, 1, alone=True)
                mix(b, 3, alone=True)
                low_xr(b, 3, alone=True)
                gate_o(b, 1, alone=True)
                low_k(b, 2, alone=True)
                low_k(b, 3, alone=True)
                gate_o(b, 2, alone=True)
                gate_o(b, 3, alone=True, add=True)

            make_silu()
            stats_a(0, 0)
            stats_a(0, 1)
            take_mod_col(0, mod_a_done)
            rows_a()
            dve.wait_ge(const_ready, 10)
            make_z(0, 0, first=True)
            make_z(0, 1, first=True)
            stats_a(0, 2)
            stats_a(0, 3)
            rows_bias()
            make_z(0, 2, first=True)
            make_z(0, 3, first=True)
            prep_now(0)
            take_mod_col(1, mod_b_done)
            dve.wait_ge(wqkv_loaded, 16)
            prep_qk(0)
            rows_b()
            centre_fc()
            softmax_dif(0)
            softmax_norm(0)
            split_rk()
            stats_a(1, 0)
            stats_a(1, 1)
            make_m(0)
            make_z(1, 0)
            make_z(1, 1)
            dve.wait_ge(mod_col_ready, 2)
            dve.wait_ge(w_copied, 5)
            row_steps(0, True, True)
            with dve.Fori(1, B - 2) as b:
                row_steps(b, False, True)
            row_steps(B - 2, False, False)
            last_row(B - 1)

        @block.tensor
        def _(pe):
            mm = nc.tensor.matmul

            def mm3(dst, parts, start, stop):
                s_hi, s_lo, m_hi, m_lo = parts
                mm(dst, s_hi, m_lo, start=start, stop=False)
                mm(dst, s_hi, m_hi, start=False, stop=False)
                return mm(dst, s_lo, m_hi, start=False, stop=stop)

            def turn_c():
                pe.wait_ge(ident_ready, 1)
                pe.wait_ge(c_loaded, 16)
                for k in range(KD):
                    ins = nc.tensor.transpose(work[0][:, k * B:(k + 1) * B], c_sb[:, k * P:(k + 1) * P], ident[0:B, 0:B])
                ins.then_inc(c_turned, 1)

            def mod_columns(half):
                for n in range(4):
                    m = 6 * half + n
                    for k in range(KD):
                        ins = mm(att[0][:, (4 * half + n) * B:(4 * half + n + 1) * B], wmod_sb[:, k, m * P:(m + 1) * P],
                                 silu[:, k * B:(k + 1) * B], start=(k == 0), stop=(k == KD - 1))
                return ins

            def mod_a():
                pe.wait_ge(silu_ready, 1)
                pe.wait_ge(wmod_a_loaded, 16)
                for k in range(KD):
                    mm(work[0][0:B, :], silu[:, k * B:(k + 1) * B], wmod_sb[:, k, 0:2 * D], start=(k == 0), stop=(k == KD - 1))
                mod_columns(0).then_inc(mod_a_done, 1)

            def biases():
                pe.wait_ge(mod_col_ready, 1)
                pe.wait_ge(wqkv_loaded, 16)
                for g in range(2):
                    for k in range(KD):
                        mm(work[1 + g][0:B, :], mod_col[:, k, :], wqkv_sb[:, k, g * HD:(g + 1) * HD],
                           start=(k == 0), stop=(k == KD - 1))
                for p in range(NP):
                    for k in range(KD):
                        ins = mm(att[1][:, p * B:(p + 1) * B], wqkv_sb[:, k, QK + p * P:QK + (p + 1) * P], mod_col[:, k, :],
                                 start=(k == 0), stop=(k == KD - 1))
                ins.then_inc(bias_done, 1)

            def mod_b():
                pe.wait_ge(row8_a_read, 1)
                pe.wait_ge(wmod_b_loaded, 16)
                for n, m in enumerate((2, 5)):
                    for k in range(KD):
                        mm(work[0][0:B, n * D:(n + 1) * D], silu[:, k * B:(k + 1) * B], wmod_sb[:, k, m * D:(m + 1) * D],
                           start=(k == 0), stop=(k == KD - 1))
                mod_columns(1).then_inc(mod_b_done, 1)

            def turn_wv():
                pe.wait_ge(mod_col_ready, 2)
                pe.wait_ge(vb_ready, 1)
                for g in range(2):
                    for n in range(2):
                        p = 2 * g + n
                        for k in range(KD):
                            ins = nc.tensor.transpose(att[g][:, n * D + k * P:n * D + (k + 1) * P],
                                                      wqkv_sb[:, k, QK + p * P:QK + (p + 1) * P], ident[:])
                    ins.then_inc(w_turned, 1)

            def turn_ffn():
                pe.wait_ge(ffn_loaded, 48)
                pe.wait_ge(row8_a_ready, 1)
                pe.wait_ge(row8_b_ready, 1)
                for n in range(3):
                    for ch in range(KD):
                        for dh in range(KD):
                            ins = nc.tensor.transpose(work[n][:, ch * D + dh * P:ch * D + (dh + 1) * P],
                                                      w_ffn[:, n, dh, ch * P:(ch + 1) * P], ident[:])
                    ins.then_inc(w_turned, 1)

            def turn_and_gram(b, j, first=False):
                i = CH * b + j
                pe.wait_ge(z_ready, i + 1)
                if first or j == 1:
                    wait_past(pe, z_t_ready, 2 * i)
                elif j == 0:
                    wait_past(pe, h2_ready, 2 * CH * (b - 1))
                else:
                    pe.wait_ge(h2_ready, 2 * (CH * (b - 1) + j - 1))
                for h in range(KD):
                    for t in range(NT):
                        ins = nc.tensor.transpose(tr[h][:, t * P:(t + 1) * P], z[:, j % 2, t, h * P:(h + 1) * P], ident[:])
                    ins.then_inc(z_turned, 1)
                if j == 0 and not first:
                    pe.wait_ge(m_ready, b)
                for t in range(NT):
                    for k in range(KD):
                        ins = mm(gram[:, k * D:(k + 1) * D - k * P], z[:, j % 2, t, k * P:(k + 1) * P], z[:, j % 2, t, k * P:D],
                                 start=(j == 0 and t == 0 and k == 0), stop=(j == CH - 1 and t == NT - 1),
                                 skip_group_check=True)
                ins.then_inc(z_used, 1)

            def attention(b, j, alone=False):
                i = CH * b + j
                pe.wait_ge(m_ready, b + 1)
                pe.wait_ge(z_t_ready, 2 * i + 2)
                if not alone:
                    wait_past(pe, t_done, i)
                elif j == 1:
                    pe.wait_ge(h2_ready, 2 * CH * b)
                else:
                    pe.wait_ge(t_done, i - (j == 2))
                for q in range(2):
                    for t in (2 * q, 2 * q + 1):
                        for k in range(KD):
                            ins = mm(att_banks(j, alone)[q][:, (t % 2) * D:(t % 2 + 1) * D], z_t[:, j, k, t * P:(t + 1) * P], m_sb[:, k],
                                     start=(k == 0), stop=(k == KD - 1))
                    ins.then_inc(att_done, 1)

            def turn_z2(b, j, last=False):
                i = CH * b + j
                pe.wait_ge(z2_ready, i + 1)
                if last and j == 0:
                    pe.wait_ge(t_done, CH * b + 2)
                elif not last and j < CH - 1:
                    pe.wait_ge(z_t_ready, 2 * (i + 1 + CH) + 2)
                else:
                    wait_past(pe, h2_ready, 2 * i)
                for h in range(KD):
                    for t in range(NT):
                        ins = nc.tensor.transpose(tr[h][:, t * P:(t + 1) * P], z2[:, t, h * P:(h + 1) * P], ident[:])
                    ins.then_inc(z2_turned, 1)

            def ffn_r(b, j, alone=False):
                i = CH * b + j
                pe.wait_ge(xr_lo_ready, i + 1)
                for q in range(2):
                    if alone:
                        pe.wait_ge(t_done, CH * (b + 1))
                    elif q == 1:
                        wait_past(pe, ro_ready, 2 * i - 1)
                    for t in (2 * q, 2 * q + 1):
                        tile = slice(t * P, (t + 1) * P)
                        for ch in range(KD):
                            ins = mm3(r_banks(alone)[q][:, (t % 2) * D:(t % 2 + 1) * D],
                                      (xr_hi[:, ch, tile], xr_lo[:, ch, tile], w_rk_hi[:, 0, ch], w_rk_lo[:, 0, ch]),
                                      start=(ch == 0), stop=(ch == KD - 1))
                    ins.then_inc(r_done, 1)

            def ffn_k(b, j, alone=False):
                i = CH * b + j
                pe.wait_ge(xk_lo_ready, i + 1)
                for dh in range(KD):
                    if dh == 0 and not alone:
                        wait_past(pe, ro_ready, 2 * i)
                    elif not alone:
                        pe.wait_ge(th_ready, 2 * i + 1)
                    elif j == CH - 1:
                        pe.wait_ge(k_lo_ready, 2 * i - 1 + dh)
                    rows_dh = slice(dh * P, (dh + 1) * P)
                    for ch in range(KD):
                        ins = mm3(k_banks(alone)[dh][:],
                                  (w_rk_hi[:, 1, ch, rows_dh], w_rk_lo[:, 1, ch, rows_dh], xk_hi[:, ch], xk_lo[:, ch]),
                                  start=(ch == 0), stop=(ch == KD - 1))
                    ins.then_inc(k_done, 1)

            def ffn_out(b, j, alone=False):
                i = CH * b + j
                pe.wait_ge(now_ready, b + 1)
                pe.wait_ge(k_lo_ready, 2 * i + 2)
                pe.wait_ge(th_ready, 2 * i + 2)
                if alone and j < CH - 1:
                    pe.wait_ge(ro_ready, 2 * i)
                hi, lo = k_split(j, alone)
                for q in range(2):
                    for t in (2 * q, 2 * q + 1):
                        tile = slice(t * P, (t + 1) * P)
                        for ch in range(KD):
                            ins = mm3(o_banks(j, alone)[q][:, (t % 2) * D:(t % 2 + 1) * D],
                                      (hi[:, ch, tile], lo[:, ch, tile], wvf_hi[:, ch], wvf_lo[:, ch]),
                                      start=(ch == 0), stop=(ch == KD - 1))
                    ins.then_inc(o_done, 1)

            def turn_gram(b):
                pe.wait_ge(g_up_ready, b + 1)
                nc.tensor.transpose(gram[:, D + P:2 * D], g_sb[:, 0, P:D], ident[:]).then_inc(gram_turned, 1)

            def gram_q(b):
                pe.wait_ge(g_ready, b + 1)
                pe.wait_ge(qk_ready, b + 1)
                pe.wait_ge(edge_loaded, 32 * (b + 1))
                wait_past(pe, t_done, CH * b)
                for m in range(KD):
                    for k in range(KD):
                        ins = mm(att[m][:], g_sb[:, k, m * P:(m + 1) * P], wqk_aug[:, k, 0:HD], start=(k == 0), stop=(k == KD - 1))
                    ins.then_inc(gq_done, 1)

            def scores(b):
                pe.wait_ge(gq_ready, 2 * b + 2)
                for p in range(NP):
                    for m in range(KD):
                        ins = mm(gram[:, p * P:(p + 1) * P], gq[:, m, p * P:(p + 1) * P], wqk_aug[:, m, HD + p * P:HD + (p + 1) * P],
                                 start=(m == 0), stop=(m == KD - 1))
                ins.then_inc(score_done, 1)

            def wv_attn(b):
                pe.wait_ge(attn_ready, b + 1)
                pe.wait_ge(wv_ready, b + 1)
                for p in range(NP):
                    ins = mm(att[p // 2][:, (p % 2) * D:(p % 2 + 1) * D], attn[:, p], wv_aug[:, p], start=True, stop=True)
                    if p % 2:
                        ins.then_inc(pv_done, 1)

            def make_m(b):
                pe.wait_ge(pv_ready, 2 * b + 2)
                for k in range(KD):
                    for p in range(NP):
                        ins = mm(gram[:, k * D:(k + 1) * D], pv_t[:, p, k * P:(k + 1) * P], wfc_c[:, p], start=(p == 0), stop=(p == NP - 1))
                ins.then_inc(m_done, 1)

            def row_steps(b, first):
                n = b + 1
                attention(b, 0)
                turn_and_gram(n, 0)
                if not first:
                    ffn_r(b - 1, 3)
                    ffn_k(b - 1, 3)
                attention(b, 1)
                if not first:
                    ffn_out(b - 1, 3)
                turn_and_gram(n, 1)
                turn_z2(b, 0)
                attention(b, 2)
                turn_and_gram(n, 2)
                ffn_r(b, 0)
                ffn_k(b, 0)
                turn_z2(b, 1)
                attention(b, 3)
                ffn_out(b, 0)
                turn_and_gram(n, 3)
                turn_z2(b, 2)
                turn_gram(n)
                ffn_r(b, 1)
                ffn_k(b, 1)
                gram_q(n)
                ffn_out(b, 1)
                scores(n)
                ffn_r(b, 2)
                ffn_k(b, 2)
                wv_attn(n)
                turn_z2(b, 3)
                make_m(n)
                ffn_out(b, 2)

            def last_row(b):
                attention(b, 0)
                attention(b, 1, alone=True)
                ffn_r(b - 1, 3)
                ffn_k(b - 1, 3)
                attention(b, 2, alone=True)
                ffn_out(b - 1, 3)
                turn_z2(b, 0, last=True)
                attention(b, 3, alone=True)
                turn_z2(b, 1, last=True)
                ffn_r(b, 0)
                ffn_k(b, 0)
                turn_z2(b, 2, last=True)
                ffn_r(b, 1, alone=True)
                ffn_out(b, 0)
                ffn_k(b, 1, alone=True)
                turn_z2(b, 3, last=True)
                ffn_r(b, 2, alone=True)
                ffn_out(b, 1, alone=True)
                ffn_k(b, 2, alone=True)
                ffn_r(b, 3, alone=True)
                ffn_k(b, 3, alone=True)
                ffn_out(b, 2, alone=True)
                ffn_out(b, 3, alone=True)

            turn_c()
            mod_a()
            biases()
            turn_and_gram(0, 0, first=True)
            turn_and_gram(0, 1, first=True)
            mod_b()
            turn_and_gram(0, 2, first=True)
            turn_wv()
            turn_and_gram(0, 3, first=True)
            turn_gram(0)
            pe.wait_ge(w_copied, 2)
            gram_q(0)
            scores(0)
            turn_ffn()
            wv_attn(0)
            pe.wait_ge(fc_ready, 1)
            make_m(0)
            pe.wait_ge(w_copied, 5)
            pe.wait_ge(w_split, 1)
            row_steps(0, True)
            with pe.Fori(1, B - 1) as b:
                row_steps(b, False)
            last_row(B - 1)


_INS = ['L0_attn_x', 'L0_attn_w_qkv', 'L0_attn_b_qkv', 'L0_attn_w_fc', 'L0_attn_b_fc', 'L0_attn_gamma', 'L0_attn_beta',
        'L0_ffn_W_r', 'L0_ffn_W_k', 'L0_ffn_W_v', 'L0_ffn_mu_r', 'L0_ffn_mu_k', 'L0_c', 'L0_wmod']


def kernel(**inputs):
    import numpy as _np
    import concourse.bacc as _bacc
    from concourse import mybir as _mybir
    from concourse.bass_utils import run_bass_kernel_spmd as _run

    nc = _bacc.Bacc("TRN2", target_bir_lowering=False, num_devices=1)
    arrays, args = {}, []
    for name in _INS:
        a = _np.ascontiguousarray(inputs[name])
        arrays[f"in_{name}_dram"] = a
        args.append(nc.dram_tensor(f"in_{name}_dram", a.shape, _mybir.dt.from_np(a.dtype), kind="ExternalInput").ap())
    shape = arrays["in_L0_attn_x_dram"].shape
    args.append(nc.dram_tensor("out_0_dram", shape, _mybir.dt.float32, kind="ExternalOutput").ap())
    adaln_block(nc, *args)
    r = _run(nc, [arrays], core_ids=[0])
    return r.results[0]["out_0_dram"]
```
